# Optimizing a Trainium2 kernel written in Bass

```python
import numpy as np
import jax
import jax.numpy as jnp

def _softmax(x, axis=-1):
    return jax.nn.softmax(x, axis=axis)

def _gelu(x):
    return jax.nn.gelu(x, approximate=True)

def _silu(x):
    return jax.nn.silu(x)

def _sigmoid(x):
    return jax.nn.sigmoid(x)

def _layernorm(x, axis=-1, eps=1e-05):
    m = jnp.mean(x, axis=axis, keepdims=True)
    v = jnp.var(x, axis=axis, keepdims=True)
    return (x - m) / jnp.sqrt(v + eps)

def _scatter_add(tgt, idx, src, axis=0):
    return tgt.at[idx].add(src)

def _segment_sum(src, seg, n):
    return jax.ops.segment_sum(src, seg, n)
kernel_name = 'mk_adj_resnorm_d4_adj_r2_8b119c'

def setup_inputs(seed: int=0):
    np.random.seed(seed)
    _w = jnp.asarray

    def _rec_inputs():
        import jax
        import jax.numpy as jnp
        _gk = jax.random.key(seed)
        x = 7.22e-05 + 1 * jax.random.normal(jax.random.fold_in(_gk, 1), (64, 128, 256), jnp.float32)
        _a = jax.random.bernoulli(jax.random.fold_in(_gk, 2), 0.015625, (64, 128, 128))
        _a = jnp.logical_or(_a, jnp.swapaxes(_a, -1, -2))
        _a = jnp.logical_or(_a, jnp.eye(128, dtype=bool))
        _af = _a.astype(jnp.float32)
        _af = _af * jax.random.uniform(jax.random.fold_in(_gk, 3), (64, 128, 128), jnp.float32, 0.05, 1)
        adj = _af
        return (x, adj)
    x, adj = _rec_inputs()

    def _L0_gnn_setup():
        import jax, jax.numpy as jnp
        import numpy as np
        B, N, D = (8, 1024, 256)
        key = jax.random.key(seed)
        ks = jax.random.split(key, 8)
        scale = 0.5 / np.sqrt(D)
        x = jax.random.normal(ks[0], (B, N, D), dtype=jnp.float32)
        adj = jax.random.uniform(ks[1], (B, N, N), dtype=jnp.float32)
        Wq_w = jax.random.normal(ks[2], (D, D), dtype=jnp.float32) * scale
        Wk_w = jax.random.normal(ks[3], (D, D), dtype=jnp.float32) * scale
        Wv_w = jax.random.normal(ks[4], (D, D), dtype=jnp.float32) * scale
        Wq_b = jnp.zeros((D,), dtype=jnp.float32)
        Wk_b = jnp.zeros((D,), dtype=jnp.float32)
        Wv_b = jnp.zeros((D,), dtype=jnp.float32)
        return {'x': x, 'adj': adj, 'Wq_w': Wq_w, 'Wq_b': Wq_b, 'Wk_w': Wk_w, 'Wk_b': Wk_b, 'Wv_w': Wv_w, 'Wv_b': Wv_b}
    _L0_gnn_all = _L0_gnn_setup()
    _L0_gnn_in = {k: v for k, v in _L0_gnn_all.items() if k in ('Wq_w', 'Wq_b', 'Wk_w', 'Wk_b', 'Wv_w', 'Wv_b')}
    del _L0_gnn_all

    def _L1_gnn_setup():
        import jax, jax.numpy as jnp
        import numpy as np
        B, N, F_IN, F_HID, F_OUT = (32, 512, 256, 256, 256)

        def _gcn_layer(x, adj, W, b):
            support = jnp.einsum('bnf,fh->bnh', x, W)
            return jnp.einsum('bnm,bmh->bnh', adj, support) + b
        key = jax.random.key(seed)
        ks = jax.random.split(key, 8)

        def xavier(k, fan_in, fan_out):
            bound = float(np.sqrt(6.0 / (fan_in + fan_out)))
            return jax.random.uniform(k, (fan_in, fan_out), jnp.float32, -bound, bound)
        return {'batch_graph': jax.random.normal(ks[0], (B, N, F_IN), jnp.float32), 'adj': jax.random.uniform(ks[1], (B, N, N), jnp.float32), 'W1': xavier(ks[2], F_IN, F_HID), 'b1': jnp.zeros((F_HID,), jnp.float32), 'W2': xavier(ks[3], F_HID, F_HID), 'b2': jnp.zeros((F_HID,), jnp.float32), 'W3': xavier(ks[4], F_HID, F_OUT), 'b3': jnp.zeros((F_OUT,), jnp.float32)}
    _L1_gnn_all = _L1_gnn_setup()
    _L1_gnn_in = {k: v for k, v in _L1_gnn_all.items() if k in ('W1', 'b1', 'W2', 'b2', 'W3', 'b3')}
    del _L1_gnn_all

    def _L2_gnn_setup():
        import jax, jax.numpy as jnp
        import numpy as np
        EPS_LN = 1e-05

        def hypergraph_conv(x, adj, W, b):
            N, C, _ = adj.shape
            H = (adj != 0).astype(x.dtype)
            w = adj.reshape(N, -1)[:, :C]
            xw = jnp.einsum('ncd,hd->nch', x, W)
            Dn = jnp.einsum('nce,ne->nc', H, w)
            Dn = jnp.where(Dn > 0, 1.0 / Dn, 0.0)
            Be = H.sum(axis=1)
            Be = jnp.where(Be > 0, 1.0 / Be, 0.0)
            m = Be[:, :, None] * jnp.einsum('nce,nch->neh', H, xw)
            out = Dn[:, :, None] * jnp.einsum('nce,neh->nch', H, m)
            return out + b

        def layer_norm(x, g, b):
            mu = jnp.mean(x, axis=-1, keepdims=True)
            var = jnp.var(x, axis=-1, keepdims=True)
            return (x - mu) * jax.lax.rsqrt(var + EPS_LN) * g + b
        key = jax.random.key(seed)
        ks = jax.random.split(key, 4)
        N, C, Din, Dh, Dout = (16, 512, 256, 512, 256)
        x = jax.random.normal(ks[0], (N, C, Din), dtype=jnp.float32)
        adj = jax.random.uniform(ks[1], (N, C, C), dtype=jnp.float32, minval=0.1, maxval=1.0)
        W1 = jax.random.normal(ks[2], (Dh, Din), dtype=jnp.float32) * (1.0 / np.sqrt(Din))
        b1 = jnp.zeros((Dh,), dtype=jnp.float32)
        gamma = jnp.ones((Dh,), dtype=jnp.float32)
        beta = jnp.zeros((Dh,), dtype=jnp.float32)
        W2 = jax.random.normal(ks[3], (Dout, Dh), dtype=jnp.float32) * (1.0 / np.sqrt(Dh))
        b2 = jnp.zeros((Dout,), dtype=jnp.float32)
        return {'x': x, 'adj': adj, 'W1': W1, 'b1': b1, 'gamma': gamma, 'beta': beta, 'W2': W2, 'b2': b2}
    _L2_gnn_all = _L2_gnn_setup()
    _L2_gnn_in = {k: v for k, v in _L2_gnn_all.items() if k in ('W1', 'b1', 'gamma', 'beta', 'W2', 'b2')}
    del _L2_gnn_all

    def _L3_gnn_setup():
        import jax, jax.numpy as jnp
        import numpy as np
        EMBED_DIM = 256
        NUM_HEADS = 8
        HEAD_DIM = EMBED_DIM // NUM_HEADS
        SCALE = HEAD_DIM ** (-0.5)
        B, S = (16, 512)
        key = jax.random.key(seed)
        ks = jax.random.split(key, 12)
        init = lambda k, shape: jax.random.normal(k, shape, dtype=jnp.float32) * EMBED_DIM ** (-0.5)
        return {'x': jax.random.normal(ks[0], (B, S, EMBED_DIM), dtype=jnp.float32), 'adj_matrix': jax.random.uniform(ks[1], (B, S, S), dtype=jnp.float32), 'bond_matrix': jax.random.uniform(ks[2], (B, S, S), dtype=jnp.float32), 'Wq': init(ks[3], (EMBED_DIM, EMBED_DIM)), 'bq': jnp.zeros((EMBED_DIM,), jnp.float32), 'Wk': init(ks[4], (EMBED_DIM, EMBED_DIM)), 'bk': jnp.zeros((EMBED_DIM,), jnp.float32), 'Wv': init(ks[5], (EMBED_DIM, EMBED_DIM)), 'bv': jnp.zeros((EMBED_DIM,), jnp.float32), 'Wo': init(ks[6], (EMBED_DIM, EMBED_DIM)), 'bo': jnp.zeros((EMBED_DIM,), jnp.float32), 'seq_len': S}
    _L3_gnn_all = _L3_gnn_setup()
    _L3_gnn_in = {k: v for k, v in _L3_gnn_all.items() if k in ('Wq', 'bq', 'Wk', 'bk', 'Wv', 'bv', 'Wo', 'bo')}
    del _L3_gnn_all
    return {'x': x, 'adj': adj, 'L0_gnn_Wq_w': _L0_gnn_in['Wq_w'], 'L0_gnn_Wq_b': _L0_gnn_in['Wq_b'], 'L0_gnn_Wk_w': _L0_gnn_in['Wk_w'], 'L0_gnn_Wk_b': _L0_gnn_in['Wk_b'], 'L0_gnn_Wv_w': _L0_gnn_in['Wv_w'], 'L0_gnn_Wv_b': _L0_gnn_in['Wv_b'], 'L1_gnn_W1': _L1_gnn_in['W1'], 'L1_gnn_b1': _L1_gnn_in['b1'], 'L1_gnn_W2': _L1_gnn_in['W2'], 'L1_gnn_b2': _L1_gnn_in['b2'], 'L1_gnn_W3': _L1_gnn_in['W3'], 'L1_gnn_b3': _L1_gnn_in['b3'], 'L2_gnn_W1': _L2_gnn_in['W1'], 'L2_gnn_b1': _L2_gnn_in['b1'], 'L2_gnn_gamma': _L2_gnn_in['gamma'], 'L2_gnn_beta': _L2_gnn_in['beta'], 'L2_gnn_W2': _L2_gnn_in['W2'], 'L2_gnn_b2': _L2_gnn_in['b2'], 'L3_gnn_Wq': _L3_gnn_in['Wq'], 'L3_gnn_bq': _L3_gnn_in['bq'], 'L3_gnn_Wk': _L3_gnn_in['Wk'], 'L3_gnn_bk': _L3_gnn_in['bk'], 'L3_gnn_Wv': _L3_gnn_in['Wv'], 'L3_gnn_bv': _L3_gnn_in['bv'], 'L3_gnn_Wo': _L3_gnn_in['Wo'], 'L3_gnn_bo': _L3_gnn_in['bo']}

def reference(x, adj, L0_gnn_Wq_w, L0_gnn_Wq_b, L0_gnn_Wk_w, L0_gnn_Wk_b, L0_gnn_Wv_w, L0_gnn_Wv_b, L1_gnn_W1, L1_gnn_b1, L1_gnn_W2, L1_gnn_b2, L1_gnn_W3, L1_gnn_b3, L2_gnn_W1, L2_gnn_b1, L2_gnn_gamma, L2_gnn_beta, L2_gnn_W2, L2_gnn_b2, L3_gnn_Wq, L3_gnn_bq, L3_gnn_Wk, L3_gnn_bk, L3_gnn_Wv, L3_gnn_bv, L3_gnn_Wo, L3_gnn_bo):
    import jax
    import jax.numpy as jnp

    def _L0_gnn_ref(x, adj, Wq_w, Wq_b, Wk_w, Wk_b, Wv_w, Wv_b):
        import jax, jax.numpy as jnp
        import numpy as np
        B, N, D = (8, 1024, 256)
        query = jnp.einsum('bnd,od->bno', x, Wq_w) + Wq_b
        keyt = jnp.einsum('bnd,od->bno', x, Wk_w) + Wk_b
        value = jnp.einsum('bnd,od->bno', x, Wv_w) + Wv_b
        weight = jnp.einsum('bqd,bkd->bqk', query, keyt)
        weight = adj * jnp.exp(weight)
        weight = weight / jnp.sum(weight, axis=2, keepdims=True)
        return jnp.einsum('bqk,bkd->bqd', weight, value)

    def _L1_gnn_ref(batch_graph, adj, W1, b1, W2, b2, W3, b3):
        import jax, jax.numpy as jnp
        import numpy as np
        B, N, F_IN, F_HID, F_OUT = (32, 512, 256, 256, 256)

        def _gcn_layer(x, adj, W, b):
            support = jnp.einsum('bnf,fh->bnh', x, W)
            return jnp.einsum('bnm,bmh->bnh', adj, support) + b
        x = jax.nn.relu(_gcn_layer(batch_graph, adj, W1, b1))
        x = jax.nn.relu(_gcn_layer(x, adj, W2, b2))
        out = _gcn_layer(x, adj, W3, b3)
        return out

    def _L2_gnn_ref(x, adj, W1, b1, gamma, beta, W2, b2):
        import jax, jax.numpy as jnp
        import numpy as np
        EPS_LN = 1e-05

        def hypergraph_conv(x, adj, W, b):
            N, C, _ = adj.shape
            H = (adj != 0).astype(x.dtype)
            w = adj.reshape(N, -1)[:, :C]
            xw = jnp.einsum('ncd,hd->nch', x, W)
            Dn = jnp.einsum('nce,ne->nc', H, w)
            Dn = jnp.where(Dn > 0, 1.0 / Dn, 0.0)
            Be = H.sum(axis=1)
            Be = jnp.where(Be > 0, 1.0 / Be, 0.0)
            m = Be[:, :, None] * jnp.einsum('nce,nch->neh', H, xw)
            out = Dn[:, :, None] * jnp.einsum('nce,neh->nch', H, m)
            return out + b

        def layer_norm(x, g, b):
            mu = jnp.mean(x, axis=-1, keepdims=True)
            var = jnp.var(x, axis=-1, keepdims=True)
            return (x - mu) * jax.lax.rsqrt(var + EPS_LN) * g + b
        h = jax.nn.relu(hypergraph_conv(x, adj, W1, b1))
        h = layer_norm(h, gamma, beta)
        y = hypergraph_conv(h, adj, W2, b2)
        return y + x

    def _L3_gnn_ref(x, adj_matrix, bond_matrix, Wq, bq, Wk, bk, Wv, bv, Wo, bo, seq_len):
        import jax, jax.numpy as jnp
        import numpy as np
        EMBED_DIM = 256
        NUM_HEADS = 8
        HEAD_DIM = EMBED_DIM // NUM_HEADS
        SCALE = HEAD_DIM ** (-0.5)
        B, S = (16, 512)
        b = x.shape[0]

        def proj(W, bias):
            y = jnp.einsum('bse,fe->bsf', x, W) + bias
            return y.reshape(b, seq_len, NUM_HEADS, HEAD_DIM).transpose(0, 2, 1, 3)
        q, k, v = (proj(Wq, bq), proj(Wk, bk), proj(Wv, bv))
        scores = jnp.einsum('bhqd,bhkd->bhqk', q, k) * SCALE
        mask = (adj_matrix + bond_matrix)[:, None, :, :]
        scores = scores * mask
        attn = jax.nn.softmax(scores, axis=-1)
        ctx = jnp.einsum('bhqk,bhkd->bhqd', attn, v)
        ctx = ctx.transpose(0, 2, 1, 3).reshape(b, seq_len, EMBED_DIM)
        return jnp.einsum('bse,fe->bsf', ctx, Wo) + bo
    x = _layernorm(x + _L0_gnn_ref(x, adj, L0_gnn_Wq_w, L0_gnn_Wq_b, L0_gnn_Wk_w, L0_gnn_Wk_b, L0_gnn_Wv_w, L0_gnn_Wv_b), axis=-1)
    x = _layernorm(x + _L1_gnn_ref(x, adj, L1_gnn_W1, L1_gnn_b1, L1_gnn_W2, L1_gnn_b2, L1_gnn_W3, L1_gnn_b3), axis=-1)
    x = _layernorm(x + _L2_gnn_ref(x, adj, L2_gnn_W1, L2_gnn_b1, L2_gnn_gamma, L2_gnn_beta, L2_gnn_W2, L2_gnn_b2), axis=-1)
    x = _layernorm(x + _L3_gnn_ref(x, adj, adj, L3_gnn_Wq, L3_gnn_bq, L3_gnn_Wk, L3_gnn_bk, L3_gnn_Wv, L3_gnn_bv, L3_gnn_Wo, L3_gnn_bo, 128), axis=-1)
    return x

_drawn_inputs = setup_inputs


def setup_inputs(seed=0):
    import zlib

    import numpy as np

    out = dict(_drawn_inputs(seed))
    spreads = {'L0_gnn_Wq_b': (0.0, 0.1),
     'L0_gnn_Wk_b': (0.0, 0.8),
     'L0_gnn_Wv_b': (0.0, 0.1),
     'L1_gnn_b1': (0.0, 0.1),
     'L1_gnn_b2': (0.0, 0.1),
     'L1_gnn_b3': (0.0, 0.1),
     'L2_gnn_b1': (0.0, 0.1),
     'L2_gnn_gamma': (1.0, 0.2),
     'L2_gnn_beta': (0.0, 0.1),
     'L2_gnn_b2': (0.0, 0.1),
     'L3_gnn_bq': (0.0, 0.8),
     'L3_gnn_bk': (0.0, 0.8),
     'L3_gnn_bv': (0.0, 0.1),
     'L3_gnn_bo': (0.0, 0.1)}
    factors = {}
    for name, (base, spread) in spreads.items():
        noise = np.random.default_rng([zlib.crc32(name.encode()), seed]).standard_normal(out[name].shape)
        drawn = base * np.exp(spread * noise) if base else spread * noise
        out[name] = jnp.asarray(drawn.astype(out[name].dtype))
    for name, factor in factors.items():
        out[name] = (out[name] * factor).astype(out[name].dtype)
    return out
```

```python
from contextlib import ExitStack

import concourse.bass as bass
from concourse import mybir

F32 = mybir.dt.float32
ALU = mybir.AluOpType
ACT = mybir.ActivationFunctionType
AX = mybir.AxisListType

P = 128
D = 256
C = D // P
GB = 4
N4 = GB * P
HID = 512
HC = HID // P
HEADS = 8
DH = D // HEADS
JR = P // DH
EPS = 1e-5
ATT = 2.0 * DH ** -0.5

WEIGHTS = [
    ("Wq0", C, D), ("Wk0", C, D), ("bq0", C, 1), ("bk0", C, 1), ("b1", C, 1), ("b2", C, 1), ("bup", HC, 1), ("gamma", HC, 1),
    ("beta", HC, 1), ("bqk3", 2 * C, 1), ("Wv0T", C, D + 2), ("WdownT", HC, D + 1),
    ("W1", C, D), ("W2", C, D), ("W3", C, D), ("WupT", C, HID), ("Wqk3T", C, 2 * D), ("Wv3T", C, D), ("WoT", C, D),
]
PACKED = sum(c * n for _, c, n in WEIGHTS)
FIRST = sum(c * n for _, c, n in WEIGHTS[:12])
ROWS = ["bv0", "b3", "bdown", "bv3", "bo3"]

SCHEDULE = [
    ("B", "incidence"), ("A", "att_t"), ("B", "hyper_gram"), ("A", "att_v"), ("B", "gram_turn"), ("A", "att_scores"),
    ("B", "hyper_x"),
    ("B", "hyper_up"), ("A", "att_turn"), ("B", "hyper_down"), ("A", "att_out"), ("B", "hyper_out"),
    ("A", "gcn_ax"), ("B", "mha_xt"), ("B", "mha_qk"), ("B", "mha_v"), ("B", "mha_scores0"),
    ("A", "gcn_1"), ("A", "gcn_2s"), ("B", "mha_turn0"), ("B", "mha_ctx0"), ("A", "gcn_2a"), ("B", "mha_wo0"),
    ("B", "mha_scores1"), ("A", "gcn_3s"), ("A", "gcn_3a"), ("B", "mha_turn1"), ("B", "mha_ctx1"), ("B", "mha_wo1"),
]


def build(nc, A):
    NG = A["x"].shape[0]

    ctx = ExitStack()
    with ctx:
        def sb(name, shape):
            return ctx.enter_context(nc.sbuf_tensor(name, shape, F32))

        def sem(name):
            return ctx.enter_context(nc.semaphore(name))

        ps = ctx.enter_context(nc.psum_tensor("ps", [P, 8, 512], F32))
        ps4 = ps[:].rearrange("p k (b n) -> p k b n", b=GB)
        ps2 = ps[:].rearrange("p k (b n) -> p k b n", b=2)

        packed = sb("packed", [P, PACKED])
        w = {}
        at = 0
        for name, chunks, width in WEIGHTS:
            w[name] = packed[:, at:at + chunks * width].rearrange("p (c n) -> p c n", c=chunks)
            at += chunks * width
        wq0, wk0, w_v0 = w["Wq0"], w["Wk0"], w["Wv0T"]
        w_g1, w_g2, w_g3, w_up, w_down = w["W1"], w["W2"], w["W3"], w["WupT"], w["WdownT"]
        w_qk, w_v3, w_o = w["Wqk3T"], w["Wv3T"], w["WoT"]
        bq0, bk0, b_g1, b_g2, b_up = w["bq0"], w["bk0"], w["b1"], w["b2"], w["bup"]
        gam, bet, b_qk = w["gamma"], w["beta"], w["bqk3"]
        w_att = sb("w_att", [P, C, D])
        t0 = sb("t0", [P, C])
        rows = sb("rows", [P, len(ROWS), D])
        r_g3, r_b2, r_v3, r_o = rows[:, 1], rows[:, 2], rows[:, 3], rows[:, 4]
        r_v0 = sb("r_v0", [P, D + 2])
        r_down = sb("r_down", [P, D])
        ident = sb("ident", [P, P]); ones = sb("ones", [P, P]); rep = sb("rep", [P, C + HC, P])
        mean_mat = sb("mean_mat", [P, P])

        x = sb("x", [P, GB, D]); xT = sb("xT", [P, C, N4])
        adjA = sb("adjA", [P, GB, P]); adjTA = sb("adjTA", [P, GB, P])
        tT = sb("tT", [P, C, N4]); v0 = sb("v0", [P, GB, D + 2]); e0 = sb("e0", [P, GB, P]); p0 = sb("p0", [P, GB, P])
        p0T = sb("p0T", [P, N4]); rs0 = sb("rs0", [P, GB]); x0 = sb("x0", [P, GB, D])
        axT = sb("axT", [P, C, N4]); z1T = sb("z1T", [P, C, N4]); s2 = sb("s2", [P, GB, D]); z2T = sb("z2T", [P, C, N4])
        s3 = sb("s3", [P, GB, D]); x0b = sb("x0b", [P, GB, D]); x1 = sb("x1", [P, GB, D])
        adjB = sb("adjB", [P, GB, P]); adjTB = sb("adjTB", [P, GB, P])
        hT = sb("hT", [P, GB, P]); cnt = sb("cnt", [P, 3, GB]); bhT = sb("bhT", [P, GB, P + 1])
        dn = sb("dn", [P, 5, GB]); gm = sb("gm", [P, GB, P]); gmT = sb("gmT", [P, GB, P]); gxT = sb("gxT", [P, C, N4])
        upT = sb("upT", [P, HC, N4]); sq = sb("sq", [P, HC, N4]); sqs = sb("sqs", [P, 2, N4])
        mom = sb("mom", [P, GB, 2]); hv = sb("hv", [P, 4, GB]); y2 = sb("y2", [P, GB, D])
        x1d = sb("x1d", [P, GB, D]); x2 = sb("x2", [P, GB, D])
        x2T = sb("x2T", [P, C, N4]); qkT = sb("qkT", [P, 2 * C, N4]); v3 = sb("v3", [P, GB, D])
        sm = sb("sm", [P, 2, HEADS, P]); mx = sb("mx", [P, 2, 2, HEADS]); den = sb("den", [P, 2, 2, HEADS])
        pr = sb("pr", [P, 2, HEADS, P]); prT = sb("prT", [P, 2, HEADS, P]); ctxT = sb("ctxT", [P, C, 2, P])
        x2b = sb("x2b", [P, GB, D]); x3 = sb("x3", [P, GB, D])
        st = [sb(f"st{i}", [P, GB, 6]) for i in range(4)]
        mv = [sb(f"mv{i}", [P, GB, 2]) for i in range(4)]
        var = [sb(f"var{i}", [P, GB]) for i in range(4)]
        rstd = [sb(f"rstd{i}", [P, GB]) for i in range(4)]
        held = sb("held", [P, 1])
        neg_half = sb("neg_half", [P, GB])

        setup_in = sem("setup_in"); weights_in = sem("weights_in"); ident_ready = sem("ident_ready"); setup_done = sem("setup_done")
        ones_ready = sem("ones_ready"); scaled_ready = sem("scaled_ready"); setup_mm = sem("setup_mm"); consts_ready = sem("consts_ready")
        x_in = sem("x_in"); xT_in = sem("xT_in"); adjA_in = sem("adjA_in"); adjTA_in = sem("adjTA_in")
        adjB_in = sem("adjB_in"); adjTB_in = sem("adjTB_in"); out_stored = sem("out_stored")
        t_done = sem("t_done"); t_ready = sem("t_ready"); v0_done = sem("v0_done"); v0_ready = sem("v0_ready")
        s0_done = sem("s0_done"); e0_ready = sem("e0_ready"); p0_ready = sem("p0_ready")
        p0T_done = sem("p0T_done"); p0T_ready = sem("p0T_ready"); att_done = sem("att_done")
        rs0_ready = sem("rs0_ready"); res0_ready = sem("res0_ready")
        norm_step = [sem(f"norm{i}_step") for i in range(4)]
        rstd_ready = [sem(f"rstd{i}_ready") for i in range(4)]
        x0_ready = sem("x0_ready"); ax_done = sem("ax_done"); ax_ready = sem("ax_ready")
        z1_done = sem("z1_done"); z1_ready = sem("z1_ready"); s2_done = sem("s2_done"); s2_ready = sem("s2_ready")
        z2_done = sem("z2_done"); z2_ready = sem("z2_ready"); s3_done = sem("s3_done"); s3_ready = sem("s3_ready")
        x0b_ready = sem("x0b_ready"); gcn_done = sem("gcn_done"); res1_ready = sem("res1_ready"); x1_ready = sem("x1_ready")
        inc_step = sem("inc_step"); inc_ready = sem("inc_ready"); gram_done = sem("gram_done")
        degree_step = sem("degree_step"); gm_ready = sem("gm_ready"); gmT_done = sem("gmT_done"); gmT_ready = sem("gmT_ready")
        gx_done = sem("gx_done"); gx_ready = sem("gx_ready"); up_done = sem("up_done"); up_ready = sem("up_ready")
        sq_ready = sem("sq_ready"); sqs_step = sem("sqs_step"); sqs_ready = sem("sqs_ready")
        down_done = sem("down_done"); var_step = sem("var_step"); h_rstd_ready = sem("h_rstd_ready"); y2_ready = sem("y2_ready")
        x1d_step = sem("x1d_step"); x1d_ready = sem("x1d_ready"); hyper_done = sem("hyper_done")
        res2_ready = sem("res2_ready"); x2_ready = sem("x2_ready"); x2T_done = sem("x2T_done"); x2T_ready = sem("x2T_ready")
        qk_done = sem("qk_done"); qk_ready = sem("qk_ready"); v3_done = sem("v3_done"); v3_ready = sem("v3_ready")
        s3h_done = sem("mha_scores_done"); masked_ready = sem("masked_ready"); mx_step = sem("mx_step")
        mx_ready = sem("mx_ready"); exp_ready = sem("exp_ready"); den_step = sem("den_step"); pr_ready = sem("pr_ready")
        prT_done = sem("prT_done"); prT_act = sem("prT_even_ready"); prT_dve = sem("prT_odd_ready")
        ctx_done = sem("ctx_done"); ctx_ready = sem("ctx_ready"); x2b_ready = sem("x2b_ready")
        wo_done = sem("wo_done"); res3_ready = sem("res3_ready"); x3_ready = sem("x3_ready")

        block = ctx.enter_context(nc.Block())

        def run(eng, A_steps, B_steps):
            def both(ga, gb):
                for half, name in SCHEDULE:
                    steps, g = (A_steps, ga) if half == "A" else (B_steps, gb)
                    if g is not None and name in steps:
                        steps[name](g)
            both(0, None)
            both(1, 0)
            with eng.Fori(2, NG) as g:
                both(g, g - 1)
            both(None, NG - 1)

        def first(g):
            return isinstance(g, int) and g == 0

        @block.sync
        def _(sp):
            sp.dma_start(packed[:, 0:FIRST], A["weights"][:, 0:FIRST]).then_inc(setup_in, 16)
            sp.dma_start(rows[:], A["rows"].partition_broadcast(P)).then_inc(setup_in, 16)
            sp.dma_start(xT[:], A["xT"][0]).then_inc(xT_in, 16)
            sp.dma_start(adjA[:], A["adj"][0]).then_inc(adjA_in, 16)
            sp.dma_start(x[:], A["x"][0]).then_inc(x_in, 16)
            sp.dma_start(adjTA[:], A["adjT"][0]).then_inc(adjTA_in, 16)
            sp.dma_start(packed[:, FIRST:PACKED], A["weights"][:, FIRST:PACKED]).then_inc(weights_in, 16)
            sp.dma_start(adjTB[:], A["adjT"][0]).then_inc(adjTB_in, 16)
            sp.dma_start(adjB[:], A["adj"][0]).then_inc(adjB_in, 16)

            def next_xT(g):
                sp.wait_ge(s0_done, g + 1)
                sp.dma_start(xT[:], A["xT"][g + 1]).then_inc(xT_in, 16)

            def next_adjA(g):
                sp.wait_ge(p0_ready, GB * g + GB)
                sp.dma_start(adjA[:], A["adj"][g + 1]).then_inc(adjA_in, 16)

            def next_x(g):
                sp.wait_ge(res0_ready, GB * g + GB)
                sp.dma_start(x[:], A["x"][g + 1]).then_inc(x_in, 16)

            def next_adjTA(g):
                sp.wait_ge(gcn_done, 2 * g + 2)
                sp.dma_start(adjTA[:], A["adjT"][g + 1]).then_inc(adjTA_in, 16)

            def next_adjTB(g):
                sp.wait_ge(inc_ready, g + 1)
                sp.dma_start(adjTB[:], A["adjT"][g + 1]).then_inc(adjTB_in, 16)

            def next_adjB(g):
                sp.wait_ge(masked_ready, GB * g + GB)
                sp.dma_start(adjB[:], A["adj"][g + 1]).then_inc(adjB_in, 16)

            def store(g):
                sp.wait_ge(x3_ready, GB * g + GB)
                sp.dma_start(A["out"][g], x3[:]).then_inc(out_stored, 16)

            A_steps = {"att_scores": next_xT, "att_turn": next_adjA, "att_out": next_x, "gcn_3a": next_adjTA}
            B_steps = {"incidence": next_adjTB, "mha_scores1": next_adjB, "mha_wo1": store}

            def both(ga, gb):
                for half, name in SCHEDULE:
                    steps, g = (A_steps, ga) if half == "A" else (B_steps, gb)
                    if g is not None and name in steps:
                        steps[name](g)
            both(0, None)
            both(1, 0)
            with sp.Fori(2, NG - 1) as g:
                both(g, g - 1)
            both(None, NG - 2)
            store(NG - 1)
            sp.wait_ge(out_stored, 16 * NG)

        @block.tensor
        def _(pe):
            def mm(out, lhsT, rhs, k=0, n=1):
                return pe.matmul(out, lhsT, rhs, start=(k == 0), stop=(k == n - 1))

            pe.wait_ge(consts_ready, 1)
            for m in range(C):
                for o in range(C):
                    mm(ps[:, m, 0:D], wq0[:, o, m * P:(m + 1) * P], wk0[:, o, :], o, C)
                for o in range(C):
                    mm(ps[:, m, D:D + 1], wk0[:, o, m * P:(m + 1) * P], bq0[:, o, :], o, C)
                for o in range(C):
                    mm(ps[:, m, D + 1:D + 2], wq0[:, o, m * P:(m + 1) * P], bk0[:, o, :], o, C)
            for o in range(C):
                mm(ps[:, 2, 0:1], rep[:, o, :], bk0[:, o, :], o, C)
            for f in range(HC):
                last = mm(ps[:, 3, 0:D], rep[:, C + f, :], w_down[:, f, 0:D], f, HC)
            last.then_inc(setup_mm, 1)
            pe.wait_ge(scaled_ready, 1)
            for f in range(HC):
                last = mm(ps[:, 4, 0:D], mean_mat[:], w_down[:, f, 0:D], f, HC)
            last.then_inc(setup_mm, 1)
            pe.wait_ge(setup_done, 1)
            pe.wait_ge(ident_ready, 2)
            pe.wait_ge(weights_in, 16)

            def att_t(g):
                pe.wait_ge(xT_in, 16 * g + 16)
                for m in range(C):
                    for c in range(C):
                        last = mm(ps[:, m, :], w_att[:, c, m * P:(m + 1) * P], xT[:, c, :], c, C)
                    last.then_inc(t_done, 1)

            def att_v(g):
                for b in range(GB):
                    if b < 2:
                        if not first(g):
                            pe.wait_ge(res1_ready, 2 * g)
                    else:
                        pe.wait_ge(v0_ready, GB * g + b - 1)
                    for c in range(C):
                        last = mm(ps[:, 2 + b % 2, 0:D + 2], xT[:, c, b * P:(b + 1) * P], w_v0[:, c, :], c, C)
                    last.then_inc(v0_done, 1)

            def att_scores(g):
                pe.wait_ge(t_ready, 2 * g + 2)
                for b in range(GB):
                    for c in range(C):
                        last = mm(ps4[:, 0, b], tT[:, c, b * P:(b + 1) * P], xT[:, c, b * P:(b + 1) * P], c, C)
                last.then_inc(s0_done, 1)

            def att_turn(g):
                for b in range(GB):
                    pe.wait_ge(p0_ready, GB * g + b + 1)
                    last = pe.transpose(ps4[:, 1, b], p0[:, b, :], ident[:])
                last.then_inc(p0T_done, 1)

            def att_out(g):
                pe.wait_ge(p0T_ready, g + 1)
                for b in range(GB):
                    if b < 2:
                        pe.wait_ge(v0_ready, GB * g + GB)
                    else:
                        pe.wait_ge(res0_ready, GB * g + b - 1)
                    mm(ps[:, 2 + b % 2, 0:D + 1], p0T[:, b * P:(b + 1) * P], v0[:, b, 0:D + 1]).then_inc(att_done, 1)

            def gcn_ax(g):
                pe.wait_ge(adjTA_in, 16 * g + 16)
                for b in range(GB):
                    pe.wait_ge(x0_ready, GB * g + b + 1)
                    for c in range(C):
                        last = mm(ps4[:, c, b], x0[:, b, c * P:(c + 1) * P], adjTA[:, b, :])
                last.then_inc(ax_done, 1)

            def gcn_1(g):
                pe.wait_ge(ax_ready, 2 * g + 2)
                for m in range(C):
                    for c in range(C):
                        last = mm(ps[:, 2 + m, :], w_g1[:, c, m * P:(m + 1) * P], axT[:, c, :], c, C)
                    last.then_inc(z1_done, 1)

            def gcn_2s(g):
                pe.wait_ge(z1_ready, 2 * g + 2)
                for b in range(GB):
                    for c in range(C):
                        last = mm(ps2[:, b // 2, b % 2], z1T[:, c, b * P:(b + 1) * P], w_g2[:, c, :], c, C)
                    if b % 2:
                        last.then_inc(s2_done, 1)

            def gcn_2a(g):
                for b in range(GB):
                    pe.wait_ge(s2_ready, 2 * g + 1 + b // 2)
                    for m in range(C):
                        last = mm(ps4[:, 2 + m, b], s2[:, b, m * P:(m + 1) * P], adjTA[:, b, :])
                last.then_inc(z2_done, 1)

            def gcn_3s(g):
                pe.wait_ge(z2_ready, 2 * g + 2)
                for b in range(GB):
                    for c in range(C):
                        last = mm(ps2[:, b // 2, b % 2], z2T[:, c, b * P:(b + 1) * P], w_g3[:, c, :], c, C)
                    if b % 2:
                        last.then_inc(s3_done, 1)

            def gcn_3a(g):
                for b in range(GB):
                    pe.wait_ge(s3_ready, 2 * g + 1 + b // 2)
                    last = mm(ps2[:, 2 + b // 2, b % 2], adjTA[:, b, :], s3[:, b, :])
                    if b % 2:
                        last.then_inc(gcn_done, 1)

            def hyper_gram(g):
                pe.wait_ge(inc_ready, g + 1)
                if not first(g):
                    pe.wait_ge(res3_ready, 2 * g)
                for b in range(GB):
                    last = mm(ps[:, 4 + b // 2, (b % 2) * (P + 1):(b % 2 + 1) * (P + 1)], hT[:, b, :], bhT[:, b, :])
                last.then_inc(gram_done, 1)

            def gram_turn(g):
                for b in range(GB):
                    pe.wait_ge(gm_ready, 2 * g + 1 + b // 2)
                    last = pe.transpose(ps4[:, 6, b], gm[:, b, :], ident[:])
                last.then_inc(gmT_done, 1)

            def hyper_x(g):
                pe.wait_ge(gmT_ready, g + 1)
                for b in range(GB):
                    pe.wait_ge(x1_ready, GB * g + b + 1)
                    for c in range(C):
                        last = mm(ps4[:, 4 + c, b], x1[:, b, c * P:(c + 1) * P], gmT[:, b, :])
                last.then_inc(gx_done, 1)

            def hyper_up(g):
                pe.wait_ge(gx_ready, 2 * g + 2)
                for f in range(HC):
                    for c in range(C):
                        last = mm(ps[:, 4 + (f + 2) % 4, :], w_up[:, c, f * P:(f + 1) * P], gxT[:, c, :], c, C)
                    last.then_inc(up_done, 1)

            def hyper_down(g):
                def main(b):
                    for f in range(HC):
                        mm(ps[:, 4 + (b + 2) % 4, 0:D + 1], upT[:, f, b * P:(b + 1) * P], w_down[:, f, :], f, HC)

                def square(b):
                    mm(ps[:, 4 + (b + 2) % 4, D + 1:D + 2], sqs[:, 0, b * P:(b + 1) * P], mean_mat[:, 0:1]).then_inc(down_done, 1)

                pe.wait_ge(up_ready, 4 * g + 4)
                main(0)
                main(1)
                pe.wait_ge(sqs_ready, g + 1)
                square(0)
                square(1)
                for b in range(2, GB):
                    main(b)
                    square(b)

            def hyper_out(g):
                for b in range(GB):
                    pe.wait_ge(y2_ready, GB * g + b + 1)
                    last = mm(ps2[:, 6 + b // 2, b % 2], gmT[:, b, :], y2[:, b, :])
                    if b % 2:
                        last.then_inc(hyper_done, 1)

            def mha_xt(g):
                for b in range(GB):
                    pe.wait_ge(x2_ready, GB * g + b + 1)
                    for c in range(C):
                        last = pe.transpose(ps4[:, 4 + c, b], x2[:, b, c * P:(c + 1) * P], ident[:])
                last.then_inc(x2T_done, 1)

            def mha_qk(g):
                pe.wait_ge(x2T_ready, 2 * g + 2)
                for m in range(2 * C):
                    for c in range(C):
                        last = mm(ps[:, 4 + (m + 2) % 4, :], w_qk[:, c, m * P:(m + 1) * P], x2T[:, c, :], c, C)
                    last.then_inc(qk_done, 1)

            def mha_v(g):
                for b in range(GB):
                    pe.wait_ge(qk_ready, 4 * g + 1 + b // 2)
                    for c in range(C):
                        last = mm(ps2[:, 6 + b // 2, b % 2], x2T[:, c, b * P:(b + 1) * P], w_v3[:, c, :], c, C)
                    if b % 2:
                        last.then_inc(v3_done, 1)

            def mha_scores(g, pair):
                if pair == 0:
                    pe.wait_ge(qk_ready, 4 * g + 4)
                    pe.wait_ge(v3_ready, 2 * g + 2)
                else:
                    pe.wait_ge(res3_ready, 2 * g + 1)
                for bb in range(2):
                    b = 2 * pair + bb
                    for i in range(C):
                        for j in range(JR):
                            rows = slice(j * DH, (j + 1) * DH)
                            last = mm(ps4[:, 4 + j, 2 * bb + i], qkT[rows, i, b * P:(b + 1) * P], qkT[rows, C + i, b * P:(b + 1) * P])
                last.then_inc(s3h_done, 1)

            def mha_turn(g, pair):
                for bb in range(2):
                    pe.wait_ge(masked_ready, GB * g + 2 * pair + 2)
                    pe.wait_ge(pr_ready, GB * g + 2 * pair + bb + 1)
                    for k in range(HEADS):
                        last = pe.transpose(ps4[:, 4 + 2 * bb + k // 4, k % 4], pr[:, bb, k, :], ident[:])
                    last.then_inc(prT_done, 1)

            def mha_ctx(g, pair):
                pe.wait_ge(prT_act, GB * g + 2 * pair + 2)
                pe.wait_ge(prT_dve, GB * g + 2 * pair + 2)
                for bb in range(2):
                    b = 2 * pair + bb
                    for i in range(C):
                        for j in range(JR):
                            h = JR * i + j
                            last = mm(ps4[j * DH:(j + 1) * DH, 4, 2 * i + bb], v3[:, b, h * DH:(h + 1) * DH], prT[:, bb, 2 * j + i, :])
                last.then_inc(ctx_done, 1)

            def mha_wo(g, pair):
                pe.wait_ge(ctx_ready, 2 * g + pair + 1)
                for bb in range(2):
                    for i in range(C):
                        last = mm(ps2[:, 5, bb], ctxT[:, i, bb, :], w_o[:, i, :], i, C)
                last.then_inc(wo_done, 1)

            run(pe,
                {"att_t": att_t, "att_v": att_v, "att_scores": att_scores, "att_turn": att_turn, "att_out": att_out,
                 "gcn_ax": gcn_ax, "gcn_1": gcn_1, "gcn_2s": gcn_2s, "gcn_2a": gcn_2a, "gcn_3s": gcn_3s, "gcn_3a": gcn_3a},
                {"hyper_gram": hyper_gram, "gram_turn": gram_turn, "hyper_x": hyper_x, "hyper_up": hyper_up,
                 "hyper_down": hyper_down, "hyper_out": hyper_out, "mha_xt": mha_xt, "mha_qk": mha_qk, "mha_v": mha_v,
                 "mha_scores0": lambda g: mha_scores(g, 0), "mha_turn0": lambda g: mha_turn(g, 0),
                 "mha_ctx0": lambda g: mha_ctx(g, 0), "mha_wo0": lambda g: mha_wo(g, 0),
                 "mha_scores1": lambda g: mha_scores(g, 1), "mha_turn1": lambda g: mha_turn(g, 1),
                 "mha_ctx1": lambda g: mha_ctx(g, 1), "mha_wo1": lambda g: mha_wo(g, 1)})

        @block.scalar
        def _(act):
            def att_t(g):
                for m in range(C):
                    act.wait_ge(t_done, 2 * g + m + 1)
                    act.activation(tT[:, m, :], ps[:, m, :], ACT.Identity, bias=t0[:, m:m + 1]).then_inc(t_ready, 1)

            def att_scores(g):
                act.wait_ge(s0_done, g + 1)
                act.wait_ge(v0_ready, GB * g + GB)
                for b in range(GB):
                    act.activation(e0[:, b, :], ps4[:, 0, b], ACT.Exp, bias=v0[:, b, D + 1:D + 2]).then_inc(e0_ready, 1)

            def att_turn(g):
                act.wait_ge(p0T_done, g + 1)
                act.copy(p0T[:], ps[:, 1, :]).then_inc(p0T_ready, 1)

            def gcn_ax(g):
                act.wait_ge(ax_done, g + 1)
                for c in range(C):
                    act.copy(axT[:, c, :], ps[:, c, :]).then_inc(ax_ready, 1)

            def gcn_1(g):
                for m in range(C):
                    act.wait_ge(z1_done, 2 * g + m + 1)
                    act.activation(z1T[:, m, :], ps[:, 2 + m, :], ACT.Relu, bias=b_g1[:, m, :]).then_inc(z1_ready, 1)

            def gcn_2s(g):
                for k in range(2):
                    act.wait_ge(s2_done, 2 * g + k + 1)
                    act.copy(s2[:, 2 * k:2 * k + 2, :], ps2[:, k]).then_inc(s2_ready, 1)

            def gcn_2a(g):
                act.wait_ge(z2_done, g + 1)
                for m in range(C):
                    act.activation(z2T[:, m, :], ps[:, 2 + m, :], ACT.Relu, bias=b_g2[:, m, :]).then_inc(z2_ready, 1)

            def gcn_3s(g):
                for k in range(2):
                    act.wait_ge(s3_done, 2 * g + k + 1)
                    act.copy(s3[:, 2 * k:2 * k + 2, :], ps2[:, k]).then_inc(s3_ready, 1)

            def gram_turn(g):
                act.wait_ge(gmT_done, g + 1)
                act.copy(gmT[:], ps4[:, 6]).then_inc(gmT_ready, 1)

            def hyper_x(g):
                act.wait_ge(gx_done, g + 1)
                for c in range(C):
                    act.copy(gxT[:, c, :], ps[:, 4 + c, :]).then_inc(gx_ready, 1)

            def hyper_up(g):
                for f in range(HC):
                    act.wait_ge(up_done, 4 * g + f + 1)
                    act.activation(upT[:, f, :], ps[:, 4 + (f + 2) % 4, :], ACT.Relu, bias=b_up[:, f, :]).then_inc(up_ready, 1)
                for f in range(HC):
                    act.wait_ge(up_ready, 4 * g + f + 1)
                    if not first(g):
                        act.wait_ge(sqs_ready, g)
                    act.activation(sq[:, f, :], upT[:, f, :], ACT.Square).then_inc(sq_ready, 1)

            def mha_xt(g):
                act.wait_ge(x2T_done, g + 1)
                for c in range(C):
                    act.copy(x2T[:, c, :], ps[:, 4 + c, :]).then_inc(x2T_ready, 1)

            def mha_qk(g):
                for m in range(2 * C):
                    act.wait_ge(qk_done, 4 * g + m + 1)
                    act.activation(qkT[:, m, :], ps[:, 4 + (m + 2) % 4, :], ACT.Identity, bias=b_qk[:, m, :]).then_inc(qk_ready, 1)

            def mha_scores(g, pair):
                for bb in range(2):
                    act.wait_ge(mx_ready, GB * g + 2 * pair + bb + 1)
                    for k in range(HEADS):
                        act.activation(pr[:, bb, k, :], sm[:, bb, k, :], ACT.Exp, bias=mx[:, bb, 1, k:k + 1], scale=ATT,
                                       accum_out=den[:, bb, 0, k:k + 1]).then_inc(exp_ready, 1)

            def mha_turn(g, pair):
                for bb in range(2):
                    act.wait_ge(prT_done, GB * g + 2 * pair + bb + 1)
                    act.copy(prT[:, bb, 0:4, :], ps4[:, 4 + 2 * bb]).then_inc(prT_act, 1)

            def mha_ctx(g, pair):
                act.wait_ge(ctx_done, 2 * g + pair + 1)
                act.copy(ctxT[:].rearrange("p i b n -> p (i b) n"), ps4[:, 4]).then_inc(ctx_ready, 1)

            act.wait_ge(setup_done, 1)
            run(act,
                {"att_t": att_t, "att_scores": att_scores, "att_turn": att_turn, "gcn_ax": gcn_ax, "gcn_1": gcn_1,
                 "gcn_2s": gcn_2s, "gcn_2a": gcn_2a, "gcn_3s": gcn_3s},
                {"gram_turn": gram_turn, "hyper_x": hyper_x, "hyper_up": hyper_up, "mha_xt": mha_xt, "mha_qk": mha_qk,
                 "mha_scores0": lambda g: mha_scores(g, 0), "mha_turn0": lambda g: mha_turn(g, 0),
                 "mha_ctx0": lambda g: mha_ctx(g, 0), "mha_scores1": lambda g: mha_scores(g, 1),
                 "mha_turn1": lambda g: mha_turn(g, 1), "mha_ctx1": lambda g: mha_ctx(g, 1)})

        @block.vector
        def _(dve):
            dve.memset(ones[:], 1.0)
            dve.memset(mean_mat[:], 1.0 / HID)
            dve.memset(r_v0[:, D:D + 1], 1.0).then_inc(ones_ready, 1)
            dve.wait_ge(ones_ready, 1)
            dve.wait_ge(setup_in, 32)
            dve.memset(w_v0[:, :, D:D + 1], 0.0)
            dve.memset(w_down[:, :, D:D + 1], 1.0 / HID)
            for c in range(C):
                dve.tensor_scalar(rep[:, c, :], ones[:], bq0[:, c, :], None, ALU.mult)
            for f in range(HC):
                last = dve.tensor_scalar(rep[:, C + f, :], ones[:], bet[:, f, :], None, ALU.mult)
            last.then_inc(consts_ready, 1)
            dve.wait_ge(setup_mm, 1)
            for m in range(C):
                dve.tensor_copy(w_att[:, m, :], ps[:, m, 0:D])
                dve.tensor_copy(t0[:, m:m + 1], ps[:, m, D:D + 1])
                dve.tensor_copy(w_v0[:, m, D + 1:D + 2], ps[:, m, D + 1:D + 2])
            dve.tensor_copy(r_v0[:, D + 1:D + 2], ps[:, 2, 0:1])
            dve.tensor_copy(r_v0[:, 0:D], rows[:, 0])
            dve.tensor_copy(r_down[:], ps[:, 3, 0:D])
            for f in range(HC):
                last = dve.tensor_scalar(w_down[:, f, 0:D], w_down[:, f, 0:D], gam[:, f, :], None, ALU.mult)
            last.then_inc(scaled_ready, 1)
            dve.wait_ge(setup_mm, 2)
            for f in range(HC):
                last = dve.tensor_tensor(w_down[:, f, 0:D], w_down[:, f, 0:D], ps[:, 4, 0:D], ALU.subtract)
            last.then_inc(setup_done, 1)
            dve.wait_ge(setup_done, 1)

            def norm(i, g, pair, t, ready):
                base = 5 * (2 * g + pair)
                bs = slice(2 * pair, 2 * pair + 2)
                for b in (2 * pair, 2 * pair + 1):
                    dve.bn_stats(st[i][:, b, :], t[:, b, :]).then_inc(norm_step[i], 1)
                dve.wait_ge(norm_step[i], base + 2)
                dve.memset(held[:], 0.0)
                for k in range(2):
                    dve.bn_aggr(mv[i][:, 2 * pair + k, :], st[i][:, 2 * pair + k, :]).then_inc(norm_step[i], 1)
                dve.wait_ge(norm_step[i], base + 4)
                dve.tensor_scalar(var[i][:, bs], mv[i][:, bs, 1], EPS, None, ALU.add).then_inc(norm_step[i], 1)
                dve.wait_ge(rstd_ready[i], 2 * g + pair + 1)
                for b in (2 * pair, 2 * pair + 1):
                    dve.tensor_scalar(t[:, b, :], t[:, b, :], mv[i][:, b, 0:1], rstd[i][:, b:b + 1], ALU.subtract,
                                      ALU.mult).then_inc(ready, 1)

            def att_v(g):
                for b in range(GB):
                    dve.wait_ge(v0_done, GB * g + b + 1)
                    dve.tensor_tensor(v0[:, b, :], ps[:, 2 + b % 2, 0:D + 2], r_v0[:], ALU.add).then_inc(v0_ready, 1)

            def att_scores(g):
                dve.wait_ge(adjA_in, 16 * g + 16)
                for b in range(GB):
                    dve.wait_ge(e0_ready, GB * g + b + 1)
                    dve.tensor_tensor(p0[:, b, :], e0[:, b, :], adjA[:, b, :], ALU.mult).then_inc(p0_ready, 1)

            def att_out(g):
                dve.wait_ge(x_in, 16 * g + 16)
                for b in range(GB):
                    dve.wait_ge(att_done, GB * g + b + 1)
                    dve.reciprocal(rs0[:, b:b + 1], ps[:, 2 + b % 2, D:D + 1]).then_inc(rs0_ready, 1)
                    dve.wait_ge(rs0_ready, GB * g + b + 1)
                    dve.scalar_tensor_tensor(out=x0[:, b, :], in0=ps[:, 2 + b % 2, 0:D], scalar=rs0[:, b:b + 1], in1=x[:, b, :],
                                             op0=ALU.mult, op1=ALU.add).then_inc(res0_ready, 1)
                    if b % 2:
                        dve.wait_ge(res0_ready, GB * g + b + 1)
                        norm(0, g, b // 2, x0, x0_ready)

            def gcn_3a(g):
                for k in range(2):
                    dve.wait_ge(gcn_done, 2 * g + k + 1)
                    if k == 0 and not first(g):
                        dve.wait_ge(x1d_ready, g)
                        dve.wait_ge(gx_done, g)
                    dve.wait_ge(x0b_ready, g + 1)
                    dve.tensor_tensor(x1[:, 2 * k:2 * k + 2, :], ps2[:, 2 + k], x0b[:, 2 * k:2 * k + 2, :], ALU.add).then_inc(res1_ready, 1)
                    dve.wait_ge(res1_ready, 2 * g + k + 1)
                    norm(1, g, k, x1, x1_ready)

            def incidence(g):
                def step(k):
                    dve.wait_ge(inc_step, 4 * g + k)
                dve.wait_ge(adjTB_in, 16 * g + 16)
                dve.tensor_scalar(hT[:], adjTB[:], 0.0, None, ALU.not_equal).then_inc(inc_step, 1)
                dve.tensor_copy(bhT[:, :, P:P + 1], adjTB[:, :, 0:1])
                step(1)
                dve.tensor_reduce(cnt[:, 0, :], hT[:], AX.X, ALU.add).then_inc(inc_step, 1)
                step(2)
                dve.tensor_scalar(cnt[:, 1, :], cnt[:, 0, :], 1.0, None, ALU.max).then_inc(inc_step, 1)
                step(3)
                dve.reciprocal(cnt[:, 2, :], cnt[:, 1, :]).then_inc(inc_step, 1)
                step(4)
                dve.tensor_tensor(bhT[:, :, 0:P], hT[:], cnt[:, 2, :].unsqueeze(2).broadcast_to([P, GB, P]), ALU.mult).then_inc(inc_ready, 1)

            def hyper_gram(g):
                def deg(k):
                    dve.wait_ge(degree_step, 6 * g + k)
                dve.wait_ge(gram_done, g + 1)
                d = [dn[:, i, :] for i in range(5)]
                for k in range(2):
                    dve.tensor_copy(dn[:, 0, 2 * k:2 * k + 2], ps[:, 4 + k, 0:2 * P + 2].rearrange("p (b n) -> p b n", b=2)[:, :, P]).then_inc(degree_step, 1)
                deg(2)
                dve.tensor_scalar(d[1], d[0], 0.0, None, ALU.is_gt).then_inc(degree_step, 1)
                deg(3)
                dve.tensor_scalar(d[2], d[1], 0.0, None, ALU.is_equal).then_inc(degree_step, 1)
                deg(4)
                dve.scalar_tensor_tensor(out=d[3], in0=d[0], scalar=0.0, in1=d[2], op0=ALU.max, op1=ALU.add).then_inc(degree_step, 1)
                deg(5)
                dve.reciprocal(d[4], d[3]).then_inc(degree_step, 1)
                deg(6)
                for k in range(2):
                    for b in (2 * k, 2 * k + 1):
                        last = dve.tensor_scalar(gm[:, b, :], ps[:, 4 + k, (b % 2) * (P + 1):(b % 2) * (P + 1) + P],
                                                 dn[:, 4, b:b + 1], dn[:, 1, b:b + 1], ALU.mult, ALU.mult)
                    last.then_inc(gm_ready, 1)

            def hyper_down(g):
                def step(k):
                    dve.wait_ge(var_step, 8 * g + k)
                for half in range(2):
                    bs = slice(2 * half, 2 * half + 2)
                    dve.wait_ge(down_done, GB * g + 2 * half + 2)
                    k0 = 4 * half
                    for b in (2 * half, 2 * half + 1):
                        last = dve.tensor_copy(mom[:, b, :], ps[:, 4 + (b + 2) % 4, D:D + 2])
                    last.then_inc(var_step, 1)
                    step(k0 + 1)
                    dve.tensor_tensor(hv[:, 0, bs], mom[:, bs, 0], mom[:, bs, 0], ALU.mult).then_inc(var_step, 1)
                    step(k0 + 2)
                    dve.tensor_tensor(hv[:, 1, bs], mom[:, bs, 1], hv[:, 0, bs], ALU.subtract).then_inc(var_step, 1)
                    step(k0 + 3)
                    dve.tensor_scalar(hv[:, 2, bs], hv[:, 1, bs], 0.0, EPS, ALU.max, ALU.add).then_inc(var_step, 1)
                    dve.wait_ge(h_rstd_ready, 2 * g + half + 1)
                    for b in (2 * half, 2 * half + 1):
                        dve.scalar_tensor_tensor(out=y2[:, b, :], in0=ps[:, 4 + (b + 2) % 4, 0:D], scalar=hv[:, 3, b:b + 1],
                                                 in1=r_down[:], op0=ALU.mult, op1=ALU.add).then_inc(y2_ready, 1)

            def hyper_out(g):
                for k in range(2):
                    dve.wait_ge(hyper_done, 2 * g + k + 1)
                    dve.wait_ge(x1d_ready, g + 1)
                    dve.tensor_tensor(x2[:, 2 * k:2 * k + 2, :], ps2[:, 6 + k], x1d[:, 2 * k:2 * k + 2, :], ALU.add).then_inc(res2_ready, 1)
                    dve.wait_ge(res2_ready, 2 * g + k + 1)
                    norm(2, g, k, x2, x2_ready)

            def mha_v(g):
                for k in range(2):
                    dve.wait_ge(v3_done, 2 * g + k + 1)
                    dve.tensor_tensor(v3[:, 2 * k:2 * k + 2, :], ps2[:, 6 + k], r_v3[:].unsqueeze(1).broadcast_to([P, 2, D]), ALU.add).then_inc(v3_ready, 1)

            def mha_scores(g, pair):
                if pair == 0:
                    dve.wait_ge(adjB_in, 16 * g + 16)
                dve.wait_ge(s3h_done, 2 * g + pair + 1)
                for bb in range(2):
                    b = 2 * pair + bb
                    mask = adjB[:, b, :].unsqueeze(1).unsqueeze(1).broadcast_to([P, JR, C, P])
                    dve.tensor_tensor(sm[:, bb].rearrange("p (j i) n -> p j i n", i=C), ps4[:, 4:8, 2 * bb:2 * bb + 2, :], mask,
                                      ALU.mult).then_inc(masked_ready, 1)
                    dve.wait_ge(masked_ready, GB * g + b + 1)
                    dve.tensor_reduce(mx[:, bb, 0, :], sm[:, bb], AX.X, ALU.max).then_inc(mx_step, 1)
                    dve.wait_ge(mx_step, GB * g + b + 1)
                    dve.tensor_scalar(mx[:, bb, 1, :], mx[:, bb, 0, :], -ATT, None, ALU.mult).then_inc(mx_ready, 1)
                for bb in range(2):
                    b = 2 * pair + bb
                    dve.wait_ge(exp_ready, HEADS * (GB * g + b + 1))
                    dve.reciprocal(den[:, bb, 1, :], den[:, bb, 0, :]).then_inc(den_step, 1)

            def mha_turn(g, pair):
                for bb in range(2):
                    dve.wait_ge(prT_done, GB * g + 2 * pair + bb + 1)
                    dve.tensor_copy(prT[:, bb, 4:8, :], ps4[:, 5 + 2 * bb]).then_inc(prT_dve, 1)

            def mha_wo(g, pair):
                dve.wait_ge(wo_done, 2 * g + pair + 1)
                if pair == 0 and not first(g):
                    dve.wait_ge(out_stored, 16 * g)
                dve.wait_ge(x2b_ready, g + 1)
                bs = slice(2 * pair, 2 * pair + 2)
                dve.tensor_tensor(x3[:, bs, :], ps2[:, 5], x2b[:, bs, :], ALU.add).then_inc(res3_ready, 1)
                dve.wait_ge(res3_ready, 2 * g + pair + 1)
                norm(3, g, pair, x3, x3_ready)

            run(dve,
                {"att_v": att_v, "att_scores": att_scores, "att_out": att_out, "gcn_3a": gcn_3a},
                {"incidence": incidence, "hyper_gram": hyper_gram, "hyper_down": hyper_down, "hyper_out": hyper_out, "mha_v": mha_v,
                 "mha_scores0": lambda g: mha_scores(g, 0), "mha_turn0": lambda g: mha_turn(g, 0),
                 "mha_wo0": lambda g: mha_wo(g, 0), "mha_scores1": lambda g: mha_scores(g, 1),
                 "mha_turn1": lambda g: mha_turn(g, 1), "mha_wo1": lambda g: mha_wo(g, 1)})

        @block.gpsimd
        def _(pool):
            pool.memset(neg_half[:], -0.5)
            pool.memset(ident[:], 0.0).then_inc(ident_ready, 1)
            pool.wait_ge(ident_ready, 1)
            pool.affine_select(out=ident[:], in_=ident[:], compare_op=ALU.not_equal, fill=1.0, base=0, pattern=[[-1, P]],
                               channel_multiplier=1).then_inc(ident_ready, 1)
            pool.wait_ge(ident_ready, 2)

            def inv_sqrt(i, g, pair):
                pool.wait_ge(norm_step[i], 5 * (2 * g + pair) + 5)
                bs = slice(2 * pair, 2 * pair + 2)
                pool.tensor_tensor(rstd[i][:, bs], var[i][:, bs], neg_half[:, bs], ALU.pow).then_inc(rstd_ready[i], 1)

            def att_out(g):
                inv_sqrt(0, g, 0)
                inv_sqrt(0, g, 1)
                for b in range(GB):
                    pool.wait_ge(x0_ready, GB * g + b + 1)
                    last = pool.tensor_tensor(x0b[:, b, :], x0[:, b, :], r_g3[:], ALU.add)
                last.then_inc(x0b_ready, 1)

            def hyper_x(g):
                pool.wait_ge(x1_ready, GB * g + GB)
                if not first(g):
                    pool.wait_ge(res2_ready, 2 * g)
                pool.tensor_tensor(x1d[:], x1[:], x1[:], ALU.add).then_inc(x1d_step, 1)
                pool.wait_ge(x1d_step, g + 1)
                pool.tensor_tensor(x1d[:], x1d[:], r_b2[:].unsqueeze(1).broadcast_to([P, GB, D]), ALU.add).then_inc(x1d_ready, 1)

            def hyper_up(g):
                pool.wait_ge(sq_ready, 4 * g + 2)
                pool.tensor_tensor(sqs[:, 1, :], sq[:, 0, :], sq[:, 1, :], ALU.add).then_inc(sqs_step, 1)
                pool.wait_ge(sqs_step, 2 * g + 1)
                pool.wait_ge(sq_ready, 4 * g + 3)
                pool.tensor_tensor(sqs[:, 0, :], sqs[:, 1, :], sq[:, 2, :], ALU.add).then_inc(sqs_step, 1)
                pool.wait_ge(sqs_step, 2 * g + 2)
                pool.wait_ge(sq_ready, 4 * g + 4)
                pool.tensor_tensor(sqs[:, 0, :], sqs[:, 0, :], sq[:, 3, :], ALU.add).then_inc(sqs_ready, 1)

            def gcn_3a(g):
                inv_sqrt(1, g, 0)
                inv_sqrt(1, g, 1)

            def hyper_down(g):
                for half in range(2):
                    pool.wait_ge(var_step, 8 * g + 4 * half + 4)
                    bs = slice(2 * half, 2 * half + 2)
                    pool.tensor_tensor(hv[:, 3, bs], hv[:, 2, bs], neg_half[:, bs], ALU.pow).then_inc(h_rstd_ready, 1)

            def mha_wo(g, pair):
                inv_sqrt(3, g, pair)

            def hyper_out(g):
                inv_sqrt(2, g, 0)
                inv_sqrt(2, g, 1)
                pool.wait_ge(x2_ready, GB * g + GB)
                pool.tensor_tensor(x2b[:], x2[:], r_o[:].unsqueeze(1).broadcast_to([P, GB, D]), ALU.add).then_inc(x2b_ready, 1)

            def mha_scores(g, pair):
                for bb in range(2):
                    b = 2 * pair + bb
                    pool.wait_ge(den_step, GB * g + b + 1)
                    pool.tensor_tensor(pr[:, bb], pr[:, bb], den[:, bb, 1, :].unsqueeze(2).broadcast_to([P, HEADS, P]), ALU.mult).then_inc(pr_ready, 1)

            pool.wait_ge(setup_done, 1)
            run(pool, {"att_out": att_out, "gcn_3a": gcn_3a},
                {"hyper_x": hyper_x, "hyper_up": hyper_up, "hyper_down": hyper_down, "hyper_out": hyper_out,
                 "mha_wo0": lambda g: mha_wo(g, 0), "mha_wo1": lambda g: mha_wo(g, 1),
                 "mha_scores0": lambda g: mha_scores(g, 0), "mha_scores1": lambda g: mha_scores(g, 1)})


def kernel(**inputs):
    import numpy as np
    import concourse.bacc as bacc
    from concourse.bass_utils import run_bass_kernel_spmd

    v = {k: np.asarray(a) for k, a in inputs.items()}
    x, adj = v["x"], v["adj"]
    n = x.shape[0] // GB

    def grouped(a):
        return np.ascontiguousarray(a.reshape(n, GB, *a.shape[1:]).transpose(0, 2, 1, 3))

    def filled(a, k):
        return np.concatenate([a, np.zeros((a.shape[0], k), a.dtype)], axis=1)

    w = {
        "Wq0": v["L0_gnn_Wq_w"], "Wk0": v["L0_gnn_Wk_w"], "Wv0T": filled(v["L0_gnn_Wv_w"].T, 2),
        "bq0": v["L0_gnn_Wq_b"], "bk0": v["L0_gnn_Wk_b"],
        "W1": v["L1_gnn_W1"], "W2": v["L1_gnn_W2"], "W3": v["L1_gnn_W3"], "b1": v["L1_gnn_b1"], "b2": v["L1_gnn_b2"],
        "WupT": v["L2_gnn_W1"].T, "bup": v["L2_gnn_b1"], "gamma": v["L2_gnn_gamma"], "beta": v["L2_gnn_beta"],
        "WdownT": filled(v["L2_gnn_W2"].T, 1),
        "Wqk3T": np.concatenate([v["L3_gnn_Wq"].T, v["L3_gnn_Wk"].T], axis=1),
        "bqk3": np.concatenate([v["L3_gnn_bq"], v["L3_gnn_bk"]]),
        "Wv3T": v["L3_gnn_Wv"].T, "WoT": v["L3_gnn_Wo"].T,
    }
    weights = np.concatenate(
        [w[name].reshape(c, P, m).transpose(1, 0, 2).reshape(P, c * m) for name, c, m in WEIGHTS], axis=1)
    rows = np.stack([v["L0_gnn_Wv_b"], v["L1_gnn_b3"], v["L2_gnn_b2"], v["L3_gnn_bv"], v["L3_gnn_bo"]])
    xT = x.reshape(n, GB, P, C, P).transpose(0, 4, 3, 1, 2).reshape(n, P, C, N4)
    arrays = {"x": grouped(x), "xT": np.ascontiguousarray(xT), "adj": grouped(adj), "adjT": grouped(adj.transpose(0, 2, 1)),
              "weights": np.ascontiguousarray(weights), "rows": rows}

    nc = bacc.Bacc("TRN2", target_bir_lowering=False, num_devices=1)
    A = {k: nc.dram_tensor(f"in_{k}", a.shape, F32, kind="ExternalInput").ap() for k, a in arrays.items()}
    A["out"] = nc.dram_tensor("out_x", (n, P, GB, D), F32, kind="ExternalOutput").ap()
    build(nc, A)
    r = run_bass_kernel_spmd(nc, [{f"in_{k}": a for k, a in arrays.items()}], core_ids=[0])
    out = r.results[0]["out_x"]
    return out.transpose(0, 2, 1, 3).reshape(n * GB, P, D)
```

```python
from contextlib import ExitStack

import concourse.bass as bass
from concourse import mybir

F32 = mybir.dt.float32
ALU = mybir.AluOpType
ACT = mybir.ActivationFunctionType
AX = mybir.AxisListType

P = 128
D = 256
C = D // P
GB = 4
N4 = GB * P
HID = 512
HC = HID // P
HEADS = 8
DH = D // HEADS
JR = P // DH
EPS = 1e-5
ATT = 2.0 * DH ** -0.5

WEIGHTS = [
    ("Wq0", C, D), ("Wk0", C, D), ("bq0", C, 1), ("bk0", C, 1), ("b1", C, 1), ("b2", C, 1), ("bup", HC, 1), ("gamma", HC, 1),
    ("beta", HC, 1), ("bqk3", 2 * C, 1), ("Wv0T", C, D + 1), ("WdownT", HC, D + 1),
    ("W1", C, D), ("W2", C, D), ("W3", C, D), ("WupT", C, HID), ("Wqk3T", C, 2 * D), ("Wv3T", C, D), ("WoT", C, D),
]
PACKED = sum(c * n for _, c, n in WEIGHTS)
FIRST = sum(c * n for _, c, n in WEIGHTS[:12])
ROWS = ["bv0", "b3", "bdown", "bv3", "bo3"]

SCHEDULE = [
    ("A", "att_t"), ("C", "mha_xt"), ("B", "gcn_3a"), ("B", "x1_stats"), ("B", "x1_norm"), ("C", "mha_qk"),
    ("A", "incidence"), ("A", "att_v"), ("A", "att_scores"), ("C", "mha_scores0"), ("C", "mha_v0"), ("A", "att_turn"),
    ("C", "mha_max0"), ("C", "mha_exp0"), ("C", "mha_max1"), ("C", "mha_exp1"), ("C", "mha_scores1"), ("C", "mha_v1"),
    ("A", "gram"), ("C", "mha_div0"), ("C", "mha_max2"), ("A", "att_out0"), ("B", "hyper_x"), ("A", "att_out1"),
    ("C", "mha_div1"), ("A", "x0_stats"), ("A", "gram_scale"), ("A", "x0_norm"), ("C", "mha_max3"), ("C", "mha_exp2"),
    ("B", "hyper_up"), ("A", "gcn_ax"), ("C", "mha_turn0"), ("C", "mha_turn1"), ("C", "mha_div2"), ("C", "mha_exp3"),
    ("A", "gcn_1"), ("C", "mha_ctx0"), ("B", "squares"), ("A", "gcn_2s0"), ("C", "mha_div3"), ("C", "mha_wo0"),
    ("C", "mha_turn2"), ("C", "mha_turn3"), ("C", "x3_norm0"), ("A", "gcn_2s1"), ("C", "mha_ctx1"), ("B", "x1_twice"),
    ("B", "hyper_down0"), ("C", "mha_wo1"), ("B", "hyper_down1"), ("A", "gcn_2a"), ("B", "hyper_out"), ("B", "x2_stats"),
    ("B", "x2_norm"), ("C", "x3_norm1"), ("A", "gcn_3s"), ("A", "gram_turn"),
]


def build(nc, A):
    NG = A["x"].shape[0]

    ctx = ExitStack()
    with ctx:
        def sb(name, shape):
            return ctx.enter_context(nc.sbuf_tensor(name, shape, F32))

        def sem(name):
            return ctx.enter_context(nc.semaphore(name))

        ps = ctx.enter_context(nc.psum_tensor("ps", [P, 8, 512], F32))
        ps4 = ps[:].rearrange("p k (b n) -> p k b n", b=GB)
        ps2 = ps[:].rearrange("p k (b n) -> p k b n", b=2)

        packed = sb("packed", [P, PACKED])
        w = {}
        at = 0
        for name, chunks, width in WEIGHTS:
            w[name] = packed[:, at:at + chunks * width].rearrange("p (c n) -> p c n", c=chunks)
            at += chunks * width
        wq0, wk0, w_v0 = w["Wq0"], w["Wk0"], w["Wv0T"]
        w_g1, w_g2, w_g3, w_up, w_down = w["W1"], w["W2"], w["W3"], w["WupT"], w["WdownT"]
        w_qk, w_v3, w_o = w["Wqk3T"], w["Wv3T"], w["WoT"]
        bq0, bk0, b_g1, b_g2, b_up = w["bq0"], w["bk0"], w["b1"], w["b2"], w["bup"]
        gam, bet, b_qk = w["gamma"], w["beta"], w["bqk3"]
        w_att = sb("w_att", [P, C, D])
        t0 = sb("t0", [P, C])
        rows = sb("rows", [P, len(ROWS), D])
        r_v0, r_g3, r_b2, r_v3, r_o = (rows[:, i] for i in range(5))
        c0 = sb("c0", [P, 1])
        r_down = sb("r_down", [P, D])
        ident = sb("ident", [P, P]); ones = sb("ones", [P, P]); rep = sb("rep", [P, C + HC, P])
        mean_mat = sb("mean_mat", [P, P])

        x = sb("x", [P, GB, D]); xb = sb("xb", [P, GB, D]); xT = sb("xT", [P, C, N4])
        adjA = sb("adjA", [P, GB, P]); adjTA = sb("adjTA", [P, GB, P])
        tT = sb("tT", [P, C, N4]); v0 = sb("v0", [P, GB, D + 1]); off0 = sb("off0", [P, GB]); raw0 = sb("raw0", [P, GB]); e0 = sb("e0", [P, GB, P]); p0 = sb("p0", [P, GB, P])
        p0T = sb("p0T", [P, N4]); rs0 = sb("rs0", [P, GB]); x0 = sb("x0", [P, GB, D])
        axT = sb("axT", [P, C, N4]); z1T = sb("z1T", [P, C, N4]); s2 = sb("s2", [P, GB, D]); z2T = sb("z2T", [P, C, N4])
        s3 = sb("s3", [P, GB, D]); x0b = sb("x0b", [P, GB, D]); x1 = sb("x1", [P, GB, D])
        adjB = sb("adjB", [P, GB, P])
        hT = sb("hT", [P, GB, P]); cnt = sb("cnt", [P, 3, GB]); bhT = sb("bhT", [P, GB, P + 1])
        dn = sb("dn", [P, 5, GB]); gm = sb("gm", [P, GB, P]); gmT = sb("gmT", [P, GB, P]); gxT = sb("gxT", [P, C, N4])
        upT = sb("upT", [P, HC, N4]); sq = sb("sq", [P, HC, N4]); sqs = sb("sqs", [P, 2, N4])
        mom = sb("mom", [P, GB, 2]); hv = sb("hv", [P, 4, GB]); y2 = sb("y2", [P, GB, D])
        x1d = sb("x1d", [P, GB, D]); x2 = sb("x2", [P, GB, D])
        x2T = sb("x2T", [P, C, N4]); qkT = sb("qkT", [P, 2 * C, N4]); v3 = sb("v3", [P, GB, D])
        mx = sb("mx", [P, GB, 2, HEADS]); den = sb("den", [P, GB, 2, HEADS])
        pr = sb("pr", [P, GB, HEADS, P]); prT = sb("prT", [P, 2, HEADS, P]); ctxT = sb("ctxT", [P, C, 2, P])
        x2b = sb("x2b", [P, GB, D]); x3 = sb("x3", [P, GB, D])
        st = [sb(f"st{i}", [P, GB, 6]) for i in range(4)]
        mv = [sb(f"mv{i}", [P, GB, 2]) for i in range(4)]
        var = [sb(f"var{i}", [P, GB]) for i in range(4)]
        rstd = [sb(f"rstd{i}", [P, GB]) for i in range(4)]
        held = sb("held", [P, 1])
        neg_half = sb("neg_half", [P, GB])

        setup_in = sem("setup_in"); weights_in = sem("weights_in"); ident_ready = sem("ident_ready"); setup_done = sem("setup_done")
        ones_ready = sem("ones_ready"); scaled_ready = sem("scaled_ready"); setup_mm = sem("setup_mm"); consts_ready = sem("consts_ready")
        x_in = sem("x_in"); xT_in = sem("xT_in"); adjA_in = sem("adjA_in"); adjTA_in = sem("adjTA_in")
        adjB_in = sem("adjB_in"); out_stored = sem("out_stored")
        t_done = sem("t_done"); t_ready = sem("t_ready"); v0_done = sem("v0_done"); v0_ready = sem("v0_ready")
        s0_done = sem("s0_done"); e0_ready = sem("e0_ready"); p0_ready = sem("p0_ready")
        p0T_done = sem("p0T_done"); p0T_ready = sem("p0T_ready"); att_done = sem("att_done")
        rs0_ready = sem("rs0_ready"); off0_ready = sem("off0_ready"); xb_ready = sem("xb_ready"); res0_ready = sem("res0_ready")
        norm_step = [sem(f"norm{i}_step") for i in range(4)]
        rstd_ready = [sem(f"rstd{i}_ready") for i in range(4)]
        x0_ready = sem("x0_ready"); ax_done = sem("ax_done"); ax_ready = sem("ax_ready")
        z1_done = sem("z1_done"); z1_ready = sem("z1_ready"); s2_done = sem("s2_done"); s2_ready = sem("s2_ready")
        z2_done = sem("z2_done"); z2_ready = sem("z2_ready"); s3_done = sem("s3_done"); s3_ready = sem("s3_ready")
        x0b_ready = sem("x0b_ready"); gcn_done = sem("gcn_done"); res1_ready = sem("res1_ready"); x1_ready = sem("x1_ready")
        inc_step = sem("inc_step"); inc_ready = sem("inc_ready"); gram_done = sem("gram_done")
        degree_step = sem("degree_step"); gm_ready = sem("gm_ready"); gmT_done = sem("gmT_done"); gmT_ready = sem("gmT_ready")
        gx_done = sem("gx_done"); gx_ready = sem("gx_ready"); up_done = sem("up_done"); up_ready = sem("up_ready")
        sq_ready = sem("sq_ready"); sqs_step = sem("sqs_step"); sqs_ready = sem("sqs_ready")
        down_done = sem("down_done"); var_step = sem("var_step"); h_rstd_ready = sem("h_rstd_ready"); y2_ready = sem("y2_ready")
        x1d_step = sem("x1d_step"); x1d_ready = sem("x1d_ready"); hyper_done = sem("hyper_done")
        res2_ready = sem("res2_ready"); x2_ready = sem("x2_ready"); x2T_done = sem("x2T_done"); x2T_ready = sem("x2T_ready")
        qk_done = sem("qk_done"); qk_ready = sem("qk_ready"); v3_done = sem("v3_done"); v3_ready = sem("v3_ready")
        s3h_done = sem("mha_scores_done"); masked_ready = sem("masked_ready"); mx_step = sem("mx_step")
        mx_ready = sem("mx_ready"); exp_ready = sem("exp_ready"); den_step = sem("den_step"); pr_ready = sem("pr_ready")
        prT_done = sem("prT_done"); prT_act = sem("prT_even_ready"); prT_dve = sem("prT_odd_ready")
        ctx_done = sem("ctx_done"); ctx_ready = sem("ctx_ready"); x2b_ready = sem("x2b_ready")
        wo_done = sem("wo_done"); res3_ready = sem("res3_ready"); x3_ready = sem("x3_ready")

        block = ctx.enter_context(nc.Block())

        def run(eng, steps, last_in_loop=NG - 1):
            def turn(t):
                for stage, name in SCHEDULE:
                    back = "ABC".index(stage)
                    if name in steps and not (isinstance(t, int) and not 0 <= t - back < NG):
                        steps[name](t - back)
            for t in range(3):
                turn(t)
            with eng.Fori(3, last_in_loop + 1) as t:
                turn(t)
            for t in range(last_in_loop + 1, NG + 2):
                turn(t)

        def ahead(n, k, g):
            return n * (min(g + k, NG - 1) + 1) if isinstance(g, int) else n * (g + k + 1)

        def turn_bank(b):
            return 4 if b in (0, 3) else 6

        def first(g):
            return isinstance(g, int) and g == 0

        def final(g):
            return isinstance(g, int) and g == NG - 1

        @block.sync
        def _(sp):
            sp.dma_start(packed[:, 0:FIRST], A["weights"][:, 0:FIRST]).then_inc(setup_in, 16)
            sp.dma_start(rows[:], A["rows"].partition_broadcast(P)).then_inc(setup_in, 16)
            sp.dma_start(xT[:], A["xT"][0]).then_inc(xT_in, 16)
            sp.dma_start(adjA[:], A["adj"][0]).then_inc(adjA_in, 16)
            sp.dma_start(x[:], A["x"][0]).then_inc(x_in, 16)
            sp.dma_start(adjTA[:], A["adjT"][0]).then_inc(adjTA_in, 16)
            sp.dma_start(packed[:, FIRST:PACKED], A["weights"][:, FIRST:PACKED]).then_inc(weights_in, 16)
            sp.dma_start(adjB[:], A["adj"][0]).then_inc(adjB_in, 16)

            def next_xT(g):
                if not final(g):
                    sp.wait_ge(s0_done, g + 1)
                    sp.dma_start(xT[:], A["xT"][g + 1]).then_inc(xT_in, 16)

            def next_adjA(g):
                if not final(g):
                    sp.wait_ge(p0_ready, GB * g + GB)
                    sp.dma_start(adjA[:], A["adj"][g + 1]).then_inc(adjA_in, 16)

            def next_x(g):
                if not final(g):
                    sp.wait_ge(xb_ready, g + 1)
                    sp.dma_start(x[:], A["x"][g + 1]).then_inc(x_in, 16)

            def next_adjTA(g):
                if not final(g):
                    sp.wait_ge(gcn_done, 2 * g + 2)
                    sp.wait_ge(inc_ready, g + 1)
                    sp.dma_start(adjTA[:], A["adjT"][g + 1]).then_inc(adjTA_in, 16)

            def next_adjB(g):
                if not final(g):
                    sp.wait_ge(masked_ready, GB * g + GB)
                    sp.dma_start(adjB[:], A["adj"][g + 1]).then_inc(adjB_in, 16)

            def store(g):
                sp.wait_ge(x3_ready, GB * g + GB)
                sp.dma_start(A["out"][g], x3[:]).then_inc(out_stored, 16)

            run(sp, {"att_scores": next_xT, "att_turn": next_adjA, "att_v": next_x, "gcn_3a": next_adjTA,
                     "mha_scores1": next_adjB, "x3_norm1": store}, NG - 2)
            sp.wait_ge(out_stored, 16 * NG)

        @block.tensor
        def _(pe):
            def mm(out, lhsT, rhs, k=0, n=1):
                return pe.matmul(out, lhsT, rhs, start=(k == 0), stop=(k == n - 1))

            pe.wait_ge(consts_ready, 1)
            for m in range(C):
                for o in range(C):
                    mm(ps[:, m, 0:D], wq0[:, o, m * P:(m + 1) * P], wk0[:, o, :], o, C)
                for o in range(C):
                    mm(ps[:, m, D:D + 1], wk0[:, o, m * P:(m + 1) * P], bq0[:, o, :], o, C)
                for o in range(C):
                    mm(ps[:, m, D + 1:D + 2], wq0[:, o, m * P:(m + 1) * P], bk0[:, o, :], o, C)
            for o in range(C):
                mm(ps[:, 2, 0:1], rep[:, o, :], bk0[:, o, :], o, C)
            for f in range(HC):
                last = mm(ps[:, 3, 0:D], rep[:, C + f, :], w_down[:, f, 0:D], f, HC)
            last.then_inc(setup_mm, 1)
            pe.wait_ge(scaled_ready, 1)
            for f in range(HC):
                last = mm(ps[:, 4, 0:D], mean_mat[:], w_down[:, f, 0:D], f, HC)
            last.then_inc(setup_mm, 1)
            pe.wait_ge(setup_done, 1)
            pe.wait_ge(ident_ready, 2)
            pe.wait_ge(weights_in, 16)

            def att_t(g):
                pe.wait_ge(xT_in, 16 * g + 16)
                for m in range(C):
                    if not first(g):
                        pe.wait_ge(s3_ready, 2 * g - 1 + m)
                    for c in range(C):
                        last = mm(ps[:, m, :], w_att[:, c, m * P:(m + 1) * P], xT[:, c, :], c, C)
                    last.then_inc(t_done, 1)

            def att_v(g):
                for b in range(GB):
                    if b < 2:
                        if not first(g):
                            pe.wait_ge(res1_ready, 2 * g)
                    else:
                        pe.wait_ge(v0_ready, GB * g + b - 1)
                    for c in range(C):
                        last = mm(ps[:, 2 + b % 2, 0:D + 1], xT[:, c, b * P:(b + 1) * P], w_v0[:, c, :], c, C)
                    last.then_inc(v0_done, 1)

            def att_scores(g):
                pe.wait_ge(t_ready, 2 * g + 2)
                for b in range(GB):
                    for c in range(C):
                        last = mm(ps4[:, 0, b], tT[:, c, b * P:(b + 1) * P], xT[:, c, b * P:(b + 1) * P], c, C)
                last.then_inc(s0_done, 1)

            def att_turn(g):
                for b in range(GB):
                    pe.wait_ge(p0_ready, GB * g + b + 1)
                    last = pe.transpose(ps4[:, 1, b], p0[:, b, :], ident[:])
                last.then_inc(p0T_done, 1)

            def att_out(g, pair):
                pe.wait_ge(p0T_ready, g + 1)
                for b in (2 * pair, 2 * pair + 1):
                    if pair == 0:
                        pe.wait_ge(v0_ready, GB * g + GB)
                        if not (isinstance(g, int) and g < 2):
                            pe.wait_ge(v3_ready, 2 * g - 3 + b)
                    else:
                        pe.wait_ge(res0_ready, GB * g + b - 1)
                    mm(ps[:, 2 + b % 2, 0:D + 1], p0T[:, b * P:(b + 1) * P], v0[:, b, 0:D + 1]).then_inc(att_done, 1)

            def gcn_ax(g):
                pe.wait_ge(adjTA_in, 16 * g + 16)
                pe.wait_ge(gm_ready, 2 * g + 2)
                for b in range(GB):
                    pe.wait_ge(x0_ready, GB * g + b + 1)
                    for c in range(C):
                        last = mm(ps4[:, c, b], x0[:, b, c * P:(c + 1) * P], adjTA[:, b, :])
                last.then_inc(ax_done, 1)

            def gcn_1(g):
                pe.wait_ge(ax_ready, 2 * g + 2)
                for m in range(C):
                    for c in range(C):
                        last = mm(ps[:, 2 + m, :], w_g1[:, c, m * P:(m + 1) * P], axT[:, c, :], c, C)
                    last.then_inc(z1_done, 1)

            def gcn_2s(g, pair):
                pe.wait_ge(z1_ready, 2 * g + 2)
                for b in (2 * pair, 2 * pair + 1):
                    for c in range(C):
                        last = mm(ps2[:, b // 2, b % 2], z1T[:, c, b * P:(b + 1) * P], w_g2[:, c, :], c, C)
                    if b % 2:
                        last.then_inc(s2_done, 1)

            def gcn_2a(g):
                for b in range(GB):
                    pe.wait_ge(s2_ready, 2 * g + 1 + b // 2)
                    for m in range(C):
                        last = mm(ps4[:, 2 + m, b], s2[:, b, m * P:(m + 1) * P], adjTA[:, b, :])
                last.then_inc(z2_done, 1)

            def gcn_3s(g):
                pe.wait_ge(z2_ready, 2 * g + 2)
                for b in range(GB):
                    for c in range(C):
                        last = mm(ps2[:, b // 2, b % 2], z2T[:, c, b * P:(b + 1) * P], w_g3[:, c, :], c, C)
                    if b % 2:
                        last.then_inc(s3_done, 1)

            def gcn_3a(g):
                for b in range(GB):
                    pe.wait_ge(s3_ready, 2 * g + 1 + b // 2)
                    if b == 2:
                        pe.wait_ge(gmT_ready, g + 1)
                    last = mm(ps2[:, 3 - b // 2, b % 2], adjTA[:, b, :], s3[:, b, :])
                    if b % 2:
                        last.then_inc(gcn_done, 1)

            def gram(g):
                pe.wait_ge(inc_ready, g + 1)
                for b in range(GB):
                    if b == 2:
                        pe.wait_ge(p0T_ready, g + 1)
                    last = mm(ps[:, b // 2, (b % 2) * (P + 1):(b % 2 + 1) * (P + 1)], hT[:, b, :], bhT[:, b, :])
                last.then_inc(gram_done, 1)

            def gram_turn(g):
                for b in range(GB):
                    pe.wait_ge(gm_ready, 2 * g + 1 + b // 2)
                    last = pe.transpose(ps4[:, 2, b], gm[:, b, :], ident[:])
                last.then_inc(gmT_done, 1)

            def hyper_x(g):
                if not first(g):
                    pe.wait_ge(masked_ready, GB * g)
                for b in range(GB):
                    pe.wait_ge(x1_ready, GB * g + b + 1)
                    for c in range(C):
                        last = mm(ps4[:, 6 + c, b], x1[:, b, c * P:(c + 1) * P], gmT[:, b, :])
                last.then_inc(gx_done, 1)

            def hyper_up(g):
                pe.wait_ge(gx_ready, 2 * g + 2)
                for f in range(HC):
                    for c in range(C):
                        last = mm(ps[:, 4 + f, :], w_up[:, c, f * P:(f + 1) * P], gxT[:, c, :], c, C)
                    last.then_inc(up_done, 1)

            def hyper_down(g, half):
                pe.wait_ge(up_ready, 4 * g + 4)
                for b in (2 * half, 2 * half + 1):
                    if b == 3 and not first(g):
                        pe.wait_ge(res3_ready, 2 * g)
                    for f in range(HC):
                        mm(ps[:, 4 + b, 0:D + 1], upT[:, f, b * P:(b + 1) * P], w_down[:, f, :], f, HC)
                pe.wait_ge(sqs_ready, g + 1)
                for b in (2 * half, 2 * half + 1):
                    mm(ps[:, 4 + b, D + 1:D + 2], sqs[:, 0, b * P:(b + 1) * P], mean_mat[:, 0:1]).then_inc(down_done, 1)

            def hyper_out(g):
                for b in range(GB):
                    pe.wait_ge(y2_ready, GB * g + b + 1)
                    last = mm(ps2[:, 4 + b // 2, b % 2], gmT[:, b, :], y2[:, b, :])
                    if b % 2:
                        last.then_inc(hyper_done, 1)

            def mha_xt(g):
                for b in range(GB):
                    pe.wait_ge(x2_ready, GB * g + b + 1)
                    for c in range(C):
                        last = pe.transpose(ps4[:, 6 + c, b], x2[:, b, c * P:(c + 1) * P], ident[:])
                last.then_inc(x2T_done, 1)

            def mha_qk(g):
                pe.wait_ge(x2T_ready, 2 * g + 2)
                for m in range(2 * C):
                    for c in range(C):
                        last = mm(ps[:, 4 + m, :], w_qk[:, c, m * P:(m + 1) * P], x2T[:, c, :], c, C)
                    last.then_inc(qk_done, 1)

            def mha_v(g, pair):
                if pair == 0:
                    pe.wait_ge(res1_ready, ahead(2, 1, g))
                    pe.wait_ge(v0_ready, ahead(GB, 2, g))
                for b in (2 * pair, 2 * pair + 1):
                    for c in range(C):
                        last = mm(ps2[:, 2 + b // 2, b % 2], x2T[:, c, b * P:(b + 1) * P], w_v3[:, c, :], c, C)
                    if b % 2:
                        last.then_inc(v3_done, 1)

            def mha_scores(g, pair):
                if pair == 0:
                    pe.wait_ge(qk_ready, 4 * g + 4)
                else:
                    pe.wait_ge(masked_ready, GB * g + 2)
                for bb in range(2):
                    b = 2 * pair + bb
                    for i in range(C):
                        for j in range(JR):
                            rows = slice(j * DH, (j + 1) * DH)
                            last = mm(ps4[:, 4 + j, 2 * bb + i], qkT[rows, i, b * P:(b + 1) * P], qkT[rows, C + i, b * P:(b + 1) * P])
                last.then_inc(s3h_done, 1)

            def mha_turn(g, b):
                pe.wait_ge(pr_ready, GB * g + b + 1)
                if b < 2:
                    pe.wait_ge(up_ready, ahead(4, 1, g) - 2 + 2 * b)
                if b == 3:
                    pe.wait_ge(res3_ready, 2 * g + 1)
                for k in range(HEADS):
                    last = pe.transpose(ps4[:, turn_bank(b) + k // 4, k % 4], pr[:, b, k, :], ident[:])
                last.then_inc(prT_done, 1)

            def mha_ctx(g, pair):
                pe.wait_ge(v3_ready, 2 * g + pair + 1)
                pe.wait_ge(prT_act, GB * g + 2 * pair + 2)
                pe.wait_ge(prT_dve, GB * g + 2 * pair + 2)
                for bb in range(2):
                    b = 2 * pair + bb
                    for i in range(C):
                        for j in range(JR):
                            h = JR * i + j
                            last = mm(ps4[j * DH:(j + 1) * DH, 4 + 2 * pair, 2 * i + bb], v3[:, b, h * DH:(h + 1) * DH],
                                      prT[:, bb, 2 * j + i, :])
                last.then_inc(ctx_done, 1)

            def mha_wo(g, pair):
                pe.wait_ge(ctx_ready, 2 * g + pair + 1)
                for bb in range(2):
                    for i in range(C):
                        last = mm(ps2[:, 5 + 2 * pair, bb], ctxT[:, i, bb, :], w_o[:, i, :], i, C)
                last.then_inc(wo_done, 1)

            run(pe, {
                "att_t": att_t, "att_v": att_v, "att_scores": att_scores, "att_turn": att_turn, "att_out0": lambda g: att_out(g, 0), "att_out1": lambda g: att_out(g, 1),
                "gcn_ax": gcn_ax, "gram": gram, "gcn_1": gcn_1, "gram_turn": gram_turn, "gcn_2a": gcn_2a,
                "gcn_2s0": lambda g: gcn_2s(g, 0), "gcn_2s1": lambda g: gcn_2s(g, 1),
                "gcn_3s": gcn_3s, "gcn_3a": gcn_3a, "hyper_x": hyper_x, "hyper_up": hyper_up,
                "hyper_down0": lambda g: hyper_down(g, 0), "hyper_down1": lambda g: hyper_down(g, 1),
                "hyper_out": hyper_out, "mha_xt": mha_xt, "mha_qk": mha_qk,
                "mha_v0": lambda g: mha_v(g, 0), "mha_v1": lambda g: mha_v(g, 1),
                "mha_scores0": lambda g: mha_scores(g, 0), "mha_scores1": lambda g: mha_scores(g, 1),
                "mha_turn0": lambda g: mha_turn(g, 0), "mha_turn1": lambda g: mha_turn(g, 1),
                "mha_turn2": lambda g: mha_turn(g, 2), "mha_turn3": lambda g: mha_turn(g, 3),
                "mha_ctx0": lambda g: mha_ctx(g, 0), "mha_ctx1": lambda g: mha_ctx(g, 1),
                "mha_wo0": lambda g: mha_wo(g, 0), "mha_wo1": lambda g: mha_wo(g, 1)})

        @block.scalar
        def _(act):
            def att_t(g):
                for m in range(C):
                    act.wait_ge(t_done, 2 * g + m + 1)
                    act.activation(tT[:, m, :], ps[:, m, :], ACT.Identity, bias=t0[:, m:m + 1]).then_inc(t_ready, 1)

            def att_v(g):
                for b in range(GB):
                    act.wait_ge(v0_done, GB * g + b + 1)
                    act.copy(raw0[:, b:b + 1], ps[:, 2 + b % 2, D:D + 1])
                    act.copy(v0[:, b, 0:D], ps[:, 2 + b % 2, 0:D]).then_inc(v0_ready, 1)
                act.wait_ge(v0_ready, GB * g + GB)
                act.activation(off0[:], raw0[:], ACT.Identity, bias=c0[:]).then_inc(off0_ready, 1)

            def att_scores(g):
                act.wait_ge(s0_done, g + 1)
                act.wait_ge(off0_ready, g + 1)
                for b in range(GB):
                    act.activation(e0[:, b, :], ps4[:, 0, b], ACT.Exp, bias=off0[:, b:b + 1]).then_inc(e0_ready, 1)

            def gcn_ax(g):
                act.wait_ge(ax_done, g + 1)
                for c in range(C):
                    act.copy(axT[:, c, :], ps[:, c, :]).then_inc(ax_ready, 1)

            def gcn_1(g):
                for m in range(C):
                    act.wait_ge(z1_done, 2 * g + m + 1)
                    act.activation(z1T[:, m, :], ps[:, 2 + m, :], ACT.Relu, bias=b_g1[:, m, :]).then_inc(z1_ready, 1)

            def gcn_2s(g, k):
                act.wait_ge(s2_done, 2 * g + k + 1)
                act.copy(s2[:, 2 * k:2 * k + 2, :], ps2[:, k]).then_inc(s2_ready, 1)

            def gcn_2a(g):
                act.wait_ge(z2_done, g + 1)
                for m in range(C):
                    act.activation(z2T[:, m, :], ps[:, 2 + m, :], ACT.Relu, bias=b_g2[:, m, :]).then_inc(z2_ready, 1)

            def gcn_3s(g):
                for k in range(2):
                    act.wait_ge(s3_done, 2 * g + k + 1)
                    act.copy(s3[:, 2 * k:2 * k + 2, :], ps2[:, k]).then_inc(s3_ready, 1)

            def gram_turn(g):
                act.wait_ge(gmT_done, g + 1)
                if not first(g):
                    act.wait_ge(hyper_done, 2 * g)
                act.copy(gmT[:], ps4[:, 2]).then_inc(gmT_ready, 1)

            def hyper_x(g):
                act.wait_ge(gx_done, g + 1)
                for c in range(C):
                    act.copy(gxT[:, c, :], ps[:, 6 + c, :]).then_inc(gx_ready, 1)

            def hyper_up(g):
                for f in range(HC):
                    act.wait_ge(up_done, 4 * g + f + 1)
                    act.activation(upT[:, f, :], ps[:, 4 + f, :], ACT.Relu, bias=b_up[:, f, :]).then_inc(up_ready, 1)

            def squares(g):
                for f in range(HC):
                    act.wait_ge(up_ready, 4 * g + f + 1)
                    if not first(g):
                        act.wait_ge(sqs_ready, g)
                    act.activation(sq[:, f, :], upT[:, f, :], ACT.Square).then_inc(sq_ready, 1)

            def mha_xt(g):
                act.wait_ge(x2T_done, g + 1)
                for c in range(C):
                    act.copy(x2T[:, c, :], ps[:, 6 + c, :]).then_inc(x2T_ready, 1)

            def mha_qk(g):
                for m in range(2 * C):
                    act.wait_ge(qk_done, 4 * g + m + 1)
                    act.activation(qkT[:, m, :], ps[:, 4 + m, :], ACT.Identity, bias=b_qk[:, m, :]).then_inc(qk_ready, 1)

            def mha_exp(g, b):
                act.wait_ge(mx_ready, GB * g + b + 1)
                for k in range(HEADS):
                    act.activation(pr[:, b, k, :], pr[:, b, k, :], ACT.Exp, bias=mx[:, b, 1, k:k + 1], scale=ATT,
                                   accum_out=den[:, b, 0, k:k + 1]).then_inc(exp_ready, 1)

            def mha_turn(g, b):
                act.wait_ge(prT_done, GB * g + b + 1)
                act.copy(prT[:, b % 2, 0:4, :], ps4[:, turn_bank(b)]).then_inc(prT_act, 1)

            def mha_ctx(g, pair):
                act.wait_ge(ctx_done, 2 * g + pair + 1)
                act.copy(ctxT[:].rearrange("p i b n -> p (i b) n"), ps4[:, 4 + 2 * pair]).then_inc(ctx_ready, 1)

            act.wait_ge(setup_done, 1)
            run(act, {
                "att_t": att_t, "att_v": att_v, "att_scores": att_scores, "gcn_ax": gcn_ax, "gcn_1": gcn_1,
                "gram_turn": gram_turn, "gcn_2a": gcn_2a, "gcn_3s": gcn_3s,
                "gcn_2s0": lambda g: gcn_2s(g, 0), "gcn_2s1": lambda g: gcn_2s(g, 1), "squares": squares,
                "hyper_x": hyper_x, "hyper_up": hyper_up, "mha_xt": mha_xt, "mha_qk": mha_qk,
                "mha_exp0": lambda g: mha_exp(g, 0), "mha_exp1": lambda g: mha_exp(g, 1),
                "mha_exp2": lambda g: mha_exp(g, 2), "mha_exp3": lambda g: mha_exp(g, 3),
                "mha_turn0": lambda g: mha_turn(g, 0), "mha_turn1": lambda g: mha_turn(g, 1),
                "mha_turn2": lambda g: mha_turn(g, 2), "mha_turn3": lambda g: mha_turn(g, 3),
                "mha_ctx0": lambda g: mha_ctx(g, 0), "mha_ctx1": lambda g: mha_ctx(g, 1)})

        @block.vector
        def _(dve):
            dve.memset(ones[:], 1.0)
            dve.memset(mean_mat[:], 1.0 / HID)
            dve.memset(v0[:, :, D:D + 1], 1.0).then_inc(ones_ready, 1)
            dve.wait_ge(ones_ready, 1)
            dve.wait_ge(setup_in, 32)
            dve.memset(w_down[:, :, D:D + 1], 1.0 / HID)
            for c in range(C):
                dve.tensor_scalar(rep[:, c, :], ones[:], bq0[:, c, :], None, ALU.mult)
            for f in range(HC):
                last = dve.tensor_scalar(rep[:, C + f, :], ones[:], bet[:, f, :], None, ALU.mult)
            last.then_inc(consts_ready, 1)
            dve.wait_ge(setup_mm, 1)
            for m in range(C):
                dve.tensor_copy(w_att[:, m, :], ps[:, m, 0:D])
                dve.tensor_copy(t0[:, m:m + 1], ps[:, m, D:D + 1])
                dve.tensor_copy(w_v0[:, m, D:D + 1], ps[:, m, D + 1:D + 2])
            dve.tensor_copy(c0[:], ps[:, 2, 0:1])
            dve.tensor_copy(r_down[:], ps[:, 3, 0:D])
            for f in range(HC):
                last = dve.tensor_scalar(w_down[:, f, 0:D], w_down[:, f, 0:D], gam[:, f, :], None, ALU.mult)
            last.then_inc(scaled_ready, 1)
            dve.wait_ge(setup_mm, 2)
            for f in range(HC):
                last = dve.tensor_tensor(w_down[:, f, 0:D], w_down[:, f, 0:D], ps[:, 4, 0:D], ALU.subtract)
            last.then_inc(setup_done, 1)
            dve.wait_ge(setup_done, 1)

            def stats(i, g, pairs, t):
                bs = slice(2 * pairs[0], 2 * pairs[-1] + 2)
                base = 5 * (2 * g + pairs[0])
                n = 2 * len(pairs)
                for b in range(bs.start, bs.stop):
                    dve.bn_stats(st[i][:, b, :], t[:, b, :]).then_inc(norm_step[i], 1)
                dve.wait_ge(norm_step[i], base + n)
                dve.memset(held[:], 0.0)
                for b in range(bs.start, bs.stop):
                    dve.bn_aggr(mv[i][:, b, :], st[i][:, b, :]).then_inc(norm_step[i], 1)
                dve.wait_ge(norm_step[i], base + 2 * n)
                dve.tensor_scalar(var[i][:, bs], mv[i][:, bs, 1], EPS, None, ALU.add).then_inc(norm_step[i], len(pairs))

            def scale(i, g, pairs, t, ready):
                dve.wait_ge(rstd_ready[i], 2 * g + pairs[-1] + 1)
                for b in range(2 * pairs[0], 2 * pairs[-1] + 2):
                    dve.tensor_scalar(t[:, b, :], t[:, b, :], mv[i][:, b, 0:1], rstd[i][:, b:b + 1], ALU.subtract,
                                      ALU.mult).then_inc(ready, 1)

            def x0_stats(g):
                dve.wait_ge(res0_ready, GB * g + GB)
                stats(0, g, (0, 1), x0)

            def x0_norm(g):
                scale(0, g, (0, 1), x0, x0_ready)

            def x1_stats(g):
                dve.wait_ge(res1_ready, 2 * g + 2)
                stats(1, g, (0, 1), x1)

            def x1_norm(g):
                scale(1, g, (0, 1), x1, x1_ready)

            def x2_stats(g):
                dve.wait_ge(res2_ready, 2 * g + 2)
                stats(2, g, (0, 1), x2)

            def x2_norm(g):
                scale(2, g, (0, 1), x2, x2_ready)

            def x3_norm(g, pair):
                dve.wait_ge(res3_ready, 2 * g + pair + 1)
                stats(3, g, (pair,), x3)
                scale(3, g, (pair,), x3, x3_ready)

            def att_scores(g):
                dve.wait_ge(adjA_in, 16 * g + 16)
                for b in range(GB):
                    dve.wait_ge(e0_ready, GB * g + b + 1)
                    dve.tensor_tensor(p0[:, b, :], e0[:, b, :], adjA[:, b, :], ALU.mult).then_inc(p0_ready, 1)

            def att_turn(g):
                dve.wait_ge(p0T_done, g + 1)
                dve.tensor_copy(p0T[:], ps[:, 1, :]).then_inc(p0T_ready, 1)

            def att_out(g, pair):
                dve.wait_ge(xb_ready, g + 1)
                for b in (2 * pair, 2 * pair + 1):
                    dve.wait_ge(att_done, GB * g + b + 1)
                    dve.reciprocal(rs0[:, b:b + 1], ps[:, 2 + b % 2, D:D + 1]).then_inc(rs0_ready, 1)
                    dve.wait_ge(rs0_ready, GB * g + b + 1)
                    dve.scalar_tensor_tensor(out=x0[:, b, :], in0=ps[:, 2 + b % 2, 0:D], scalar=rs0[:, b:b + 1], in1=xb[:, b, :],
                                             op0=ALU.mult, op1=ALU.add).then_inc(res0_ready, 1)

            def gcn_3a(g):
                for k in range(2):
                    dve.wait_ge(gcn_done, 2 * g + k + 1)
                    if k == 0 and not first(g):
                        dve.wait_ge(x1d_ready, g)
                        dve.wait_ge(gx_done, g)
                    dve.wait_ge(x0b_ready, g + 1)
                    dve.tensor_tensor(x1[:, 2 * k:2 * k + 2, :], ps2[:, 3 - k], x0b[:, 2 * k:2 * k + 2, :], ALU.add).then_inc(res1_ready, 1)

            def incidence(g):
                def step(k):
                    dve.wait_ge(inc_step, 4 * g + k)
                dve.wait_ge(adjTA_in, 16 * g + 16)
                dve.tensor_scalar(hT[:], adjTA[:], 0.0, None, ALU.not_equal).then_inc(inc_step, 1)
                dve.tensor_copy(bhT[:, :, P:P + 1], adjTA[:, :, 0:1])
                step(1)
                dve.tensor_reduce(cnt[:, 0, :], hT[:], AX.X, ALU.add).then_inc(inc_step, 1)
                step(2)
                dve.tensor_scalar(cnt[:, 1, :], cnt[:, 0, :], 1.0, None, ALU.max).then_inc(inc_step, 1)
                step(3)
                dve.reciprocal(cnt[:, 2, :], cnt[:, 1, :]).then_inc(inc_step, 1)
                step(4)
                dve.tensor_tensor(bhT[:, :, 0:P], hT[:], cnt[:, 2, :].unsqueeze(2).broadcast_to([P, GB, P]), ALU.mult).then_inc(inc_ready, 1)

            def gram_scale(g):
                def deg(k):
                    dve.wait_ge(degree_step, 6 * g + k)
                dve.wait_ge(gram_done, g + 1)
                d = [dn[:, i, :] for i in range(5)]
                for k in range(2):
                    dve.tensor_copy(dn[:, 0, 2 * k:2 * k + 2], ps[:, k, 0:2 * P + 2].rearrange("p (b n) -> p b n", b=2)[:, :, P]).then_inc(degree_step, 1)
                deg(2)
                dve.tensor_scalar(d[1], d[0], 0.0, None, ALU.is_gt).then_inc(degree_step, 1)
                deg(3)
                dve.tensor_scalar(d[2], d[1], 0.0, None, ALU.is_equal).then_inc(degree_step, 1)
                deg(4)
                dve.scalar_tensor_tensor(out=d[3], in0=d[0], scalar=0.0, in1=d[2], op0=ALU.max, op1=ALU.add).then_inc(degree_step, 1)
                deg(5)
                dve.reciprocal(d[4], d[3]).then_inc(degree_step, 1)
                deg(6)
                for k in range(2):
                    for b in (2 * k, 2 * k + 1):
                        last = dve.tensor_scalar(gm[:, b, :], ps[:, k, (b % 2) * (P + 1):(b % 2) * (P + 1) + P],
                                                 dn[:, 4, b:b + 1], dn[:, 1, b:b + 1], ALU.mult, ALU.mult)
                    last.then_inc(gm_ready, 1)

            def hyper_down(g, half):
                def step(k):
                    dve.wait_ge(var_step, 8 * g + 4 * half + k)
                bs = slice(2 * half, 2 * half + 2)
                dve.wait_ge(down_done, GB * g + 2 * half + 2)
                for b in (2 * half, 2 * half + 1):
                    last = dve.tensor_copy(mom[:, b, :], ps[:, 4 + b, D:D + 2])
                last.then_inc(var_step, 1)
                step(1)
                dve.tensor_tensor(hv[:, 0, bs], mom[:, bs, 0], mom[:, bs, 0], ALU.mult).then_inc(var_step, 1)
                step(2)
                dve.tensor_tensor(hv[:, 1, bs], mom[:, bs, 1], hv[:, 0, bs], ALU.subtract).then_inc(var_step, 1)
                step(3)
                dve.tensor_scalar(hv[:, 2, bs], hv[:, 1, bs], 0.0, EPS, ALU.max, ALU.add).then_inc(var_step, 1)
                dve.wait_ge(h_rstd_ready, 2 * g + half + 1)
                for b in (2 * half, 2 * half + 1):
                    dve.scalar_tensor_tensor(out=y2[:, b, :], in0=ps[:, 4 + b, 0:D], scalar=hv[:, 3, b:b + 1],
                                             in1=r_down[:], op0=ALU.mult, op1=ALU.add).then_inc(y2_ready, 1)

            def hyper_out(g):
                for k in range(2):
                    dve.wait_ge(hyper_done, 2 * g + k + 1)
                    dve.wait_ge(x1d_ready, g + 1)
                    dve.tensor_tensor(x2[:, 2 * k:2 * k + 2, :], ps2[:, 4 + k], x1d[:, 2 * k:2 * k + 2, :], ALU.add).then_inc(res2_ready, 1)

            def mha_v(g, k):
                dve.wait_ge(v3_done, 2 * g + k + 1)
                dve.tensor_tensor(v3[:, 2 * k:2 * k + 2, :], ps2[:, 2 + k], r_v3[:].unsqueeze(1).broadcast_to([P, 2, D]), ALU.add).then_inc(v3_ready, 1)

            def mha_scores(g, pair):
                if pair == 0:
                    dve.wait_ge(adjB_in, 16 * g + 16)
                dve.wait_ge(s3h_done, 2 * g + pair + 1)
                for bb in range(2):
                    b = 2 * pair + bb
                    mask = adjB[:, b, :].unsqueeze(1).unsqueeze(1).broadcast_to([P, JR, C, P])
                    dve.tensor_tensor(pr[:, b].rearrange("p (j i) n -> p j i n", i=C), ps4[:, 4:8, 2 * bb:2 * bb + 2, :], mask,
                                      ALU.mult).then_inc(masked_ready, 1)

            def mha_max(g, b):
                dve.wait_ge(masked_ready, GB * g + b + 1)
                dve.tensor_reduce(mx[:, b, 0, :], pr[:, b], AX.X, ALU.max).then_inc(mx_step, 1)
                dve.wait_ge(mx_step, GB * g + b + 1)
                dve.tensor_scalar(mx[:, b, 1, :], mx[:, b, 0, :], -ATT, None, ALU.mult).then_inc(mx_ready, 1)

            def mha_div(g, b):
                dve.wait_ge(exp_ready, HEADS * (GB * g + b + 1))
                dve.reciprocal(den[:, b, 1, :], den[:, b, 0, :]).then_inc(den_step, 1)

            def mha_turn(g, b):
                dve.wait_ge(prT_done, GB * g + b + 1)
                dve.tensor_copy(prT[:, b % 2, 4:8, :], ps4[:, turn_bank(b) + 1]).then_inc(prT_dve, 1)

            def mha_wo(g, pair):
                dve.wait_ge(wo_done, 2 * g + pair + 1)
                if pair == 0 and not first(g):
                    dve.wait_ge(out_stored, 16 * g)
                dve.wait_ge(x2b_ready, g + 1)
                bs = slice(2 * pair, 2 * pair + 2)
                dve.tensor_tensor(x3[:, bs, :], ps2[:, 5 + 2 * pair], x2b[:, bs, :], ALU.add).then_inc(res3_ready, 1)

            run(dve, {
                "att_scores": att_scores, "att_turn": att_turn, "incidence": incidence, "gram_scale": gram_scale,
                "att_out0": lambda g: att_out(g, 0), "att_out1": lambda g: att_out(g, 1),
                "gcn_3a": gcn_3a, "hyper_down0": lambda g: hyper_down(g, 0), "hyper_down1": lambda g: hyper_down(g, 1),
                "hyper_out": hyper_out, "mha_v0": lambda g: mha_v(g, 0), "mha_v1": lambda g: mha_v(g, 1),
                "x0_stats": x0_stats, "x1_stats": x1_stats, "x2_stats": x2_stats,
                "x0_norm": x0_norm, "x1_norm": x1_norm, "x2_norm": x2_norm,
                "x3_norm0": lambda g: x3_norm(g, 0), "x3_norm1": lambda g: x3_norm(g, 1),
                "mha_scores0": lambda g: mha_scores(g, 0), "mha_scores1": lambda g: mha_scores(g, 1),
                "mha_max0": lambda g: mha_max(g, 0), "mha_max1": lambda g: mha_max(g, 1),
                "mha_max2": lambda g: mha_max(g, 2), "mha_max3": lambda g: mha_max(g, 3),
                "mha_div0": lambda g: mha_div(g, 0), "mha_div1": lambda g: mha_div(g, 1),
                "mha_div2": lambda g: mha_div(g, 2), "mha_div3": lambda g: mha_div(g, 3),
                "mha_turn0": lambda g: mha_turn(g, 0), "mha_turn1": lambda g: mha_turn(g, 1),
                "mha_turn2": lambda g: mha_turn(g, 2), "mha_turn3": lambda g: mha_turn(g, 3),
                "mha_wo0": lambda g: mha_wo(g, 0), "mha_wo1": lambda g: mha_wo(g, 1)})

        @block.gpsimd
        def _(pool):
            pool.memset(neg_half[:], -0.5)
            pool.memset(ident[:], 0.0).then_inc(ident_ready, 1)
            pool.wait_ge(ident_ready, 1)
            pool.affine_select(out=ident[:], in_=ident[:], compare_op=ALU.not_equal, fill=1.0, base=0, pattern=[[-1, P]],
                               channel_multiplier=1).then_inc(ident_ready, 1)
            pool.wait_ge(ident_ready, 2)

            def inv_sqrt(i, g, pairs):
                pool.wait_ge(norm_step[i], 5 * (2 * g + pairs[-1]) + 5)
                bs = slice(2 * pairs[0], 2 * pairs[-1] + 2)
                pool.tensor_tensor(rstd[i][:, bs], var[i][:, bs], neg_half[:, bs], ALU.pow).then_inc(rstd_ready[i], len(pairs))

            def att_t(g):
                pool.wait_ge(x_in, 16 * g + 16)
                if not first(g):
                    pool.wait_ge(res0_ready, GB * g)
                pool.tensor_tensor(xb[:], x[:], r_v0[:].unsqueeze(1).broadcast_to([P, GB, D]), ALU.add).then_inc(xb_ready, 1)

            def x0_stats(g):
                inv_sqrt(0, g, (0, 1))

            def x1_stats(g):
                inv_sqrt(1, g, (0, 1))

            def x2_stats(g):
                inv_sqrt(2, g, (0, 1))

            def x0_norm(g):
                for b in range(GB):
                    pool.wait_ge(x0_ready, GB * g + b + 1)
                    last = pool.tensor_tensor(x0b[:, b, :], x0[:, b, :], r_g3[:], ALU.add)
                last.then_inc(x0b_ready, 1)

            def x1_twice(g):
                pool.wait_ge(x1_ready, GB * g + GB)
                if not first(g):
                    pool.wait_ge(res2_ready, 2 * g)
                pool.tensor_tensor(x1d[:], x1[:], x1[:], ALU.add).then_inc(x1d_step, 1)
                pool.wait_ge(x1d_step, g + 1)
                pool.tensor_tensor(x1d[:], x1d[:], r_b2[:].unsqueeze(1).broadcast_to([P, GB, D]), ALU.add).then_inc(x1d_ready, 1)

            def squares(g):
                pool.wait_ge(sq_ready, 4 * g + 2)
                pool.tensor_tensor(sqs[:, 1, :], sq[:, 0, :], sq[:, 1, :], ALU.add).then_inc(sqs_step, 1)
                pool.wait_ge(sqs_step, 2 * g + 1)
                pool.wait_ge(sq_ready, 4 * g + 3)
                pool.tensor_tensor(sqs[:, 0, :], sqs[:, 1, :], sq[:, 2, :], ALU.add).then_inc(sqs_step, 1)
                pool.wait_ge(sqs_step, 2 * g + 2)
                pool.wait_ge(sq_ready, 4 * g + 4)
                pool.tensor_tensor(sqs[:, 0, :], sqs[:, 0, :], sq[:, 3, :], ALU.add).then_inc(sqs_ready, 1)

            def hyper_down(g, half):
                pool.wait_ge(var_step, 8 * g + 4 * half + 4)
                bs = slice(2 * half, 2 * half + 2)
                pool.tensor_tensor(hv[:, 3, bs], hv[:, 2, bs], neg_half[:, bs], ALU.pow).then_inc(h_rstd_ready, 1)

            def x3_norm(g, pair):
                inv_sqrt(3, g, (pair,))

            def x2_norm(g):
                pool.wait_ge(x2_ready, GB * g + GB)
                pool.tensor_tensor(x2b[:], x2[:], r_o[:].unsqueeze(1).broadcast_to([P, GB, D]), ALU.add).then_inc(x2b_ready, 1)

            def mha_div(g, b):
                pool.wait_ge(den_step, GB * g + b + 1)
                pool.tensor_tensor(pr[:, b], pr[:, b], den[:, b, 1, :].unsqueeze(2).broadcast_to([P, HEADS, P]),
                                   ALU.mult).then_inc(pr_ready, 1)

            pool.wait_ge(setup_done, 1)
            run(pool, {
                "att_t": att_t, "x0_norm": x0_norm, "x2_norm": x2_norm, "x1_twice": x1_twice, "squares": squares,
                "x0_stats": x0_stats, "x1_stats": x1_stats, "x2_stats": x2_stats,
                "x3_norm0": lambda g: x3_norm(g, 0), "x3_norm1": lambda g: x3_norm(g, 1),
                "hyper_down0": lambda g: hyper_down(g, 0), "hyper_down1": lambda g: hyper_down(g, 1),
                "mha_div0": lambda g: mha_div(g, 0), "mha_div1": lambda g: mha_div(g, 1),
                "mha_div2": lambda g: mha_div(g, 2), "mha_div3": lambda g: mha_div(g, 3)})


def kernel(**inputs):
    import numpy as np
    import concourse.bacc as bacc
    from concourse.bass_utils import run_bass_kernel_spmd

    v = {k: np.asarray(a) for k, a in inputs.items()}
    x, adj = v["x"], v["adj"]
    n = x.shape[0] // GB

    def grouped(a):
        return np.ascontiguousarray(a.reshape(n, GB, *a.shape[1:]).transpose(0, 2, 1, 3))

    def filled(a, k):
        return np.concatenate([a, np.zeros((a.shape[0], k), a.dtype)], axis=1)

    w = {
        "Wq0": v["L0_gnn_Wq_w"], "Wk0": v["L0_gnn_Wk_w"], "Wv0T": filled(v["L0_gnn_Wv_w"].T, 1),
        "bq0": v["L0_gnn_Wq_b"], "bk0": v["L0_gnn_Wk_b"],
        "W1": v["L1_gnn_W1"], "W2": v["L1_gnn_W2"], "W3": v["L1_gnn_W3"], "b1": v["L1_gnn_b1"], "b2": v["L1_gnn_b2"],
        "WupT": v["L2_gnn_W1"].T, "bup": v["L2_gnn_b1"], "gamma": v["L2_gnn_gamma"], "beta": v["L2_gnn_beta"],
        "WdownT": filled(v["L2_gnn_W2"].T, 1),
        "Wqk3T": np.concatenate([v["L3_gnn_Wq"].T, v["L3_gnn_Wk"].T], axis=1),
        "bqk3": np.concatenate([v["L3_gnn_bq"], v["L3_gnn_bk"]]),
        "Wv3T": v["L3_gnn_Wv"].T, "WoT": v["L3_gnn_Wo"].T,
    }
    weights = np.concatenate(
        [w[name].reshape(c, P, m).transpose(1, 0, 2).reshape(P, c * m) for name, c, m in WEIGHTS], axis=1)
    rows = np.stack([v["L0_gnn_Wv_b"], v["L1_gnn_b3"], v["L2_gnn_b2"], v["L3_gnn_bv"], v["L3_gnn_bo"]])
    xT = x.reshape(n, GB, P, C, P).transpose(0, 4, 3, 1, 2).reshape(n, P, C, N4)
    arrays = {"x": grouped(x), "xT": np.ascontiguousarray(xT), "adj": grouped(adj), "adjT": grouped(adj.transpose(0, 2, 1)),
              "weights": np.ascontiguousarray(weights), "rows": rows}

    nc = bacc.Bacc("TRN2", target_bir_lowering=False, num_devices=1)
    A = {k: nc.dram_tensor(f"in_{k}", a.shape, F32, kind="ExternalInput").ap() for k, a in arrays.items()}
    A["out"] = nc.dram_tensor("out_x", (n, P, GB, D), F32, kind="ExternalOutput").ap()
    build(nc, A)
    r = run_bass_kernel_spmd(nc, [{f"in_{k}": a for k, a in arrays.items()}], core_ids=[0])
    out = r.results[0]["out_x"]
    return out.transpose(0, 2, 1, 3).reshape(n * GB, P, D)
```

```python
from contextlib import ExitStack

import concourse.bass as bass
from concourse import mybir

F32 = mybir.dt.float32
F32R = mybir.dt.float32r
ALU = mybir.AluOpType
ACT = mybir.ActivationFunctionType
AX = mybir.AxisListType

P = 128
D = 256
C = D // P
GB = 4
N4 = GB * P
HID = 512
HC = HID // P
HEADS = 8
DH = D // HEADS
JR = P // DH
EPS = 1e-5
ATT = 2.0 * DH ** -0.5

BIASES = [("bq0", C, 1), ("bk0", C, 1), ("b1", C, 1), ("b2", C, 1), ("bup", HC, 1), ("gamma", HC, 1), ("beta", HC, 1),
          ("bqk3", 2 * C, 1), ("bv3", C, 1)]
SETUP = [("Wq0", C, D), ("Wk0", C, D), ("Wv0T", C, D + 2), ("WdownT", HC, D + 2)]
IN_PR = [("W1", C, D), ("W2", C, D)]
IN_QKT = [("WupT", C, HID), ("Wqk3T", C, 2 * D)]
IN_UPT = [("W3", C, D), ("Wv3T", C, D), ("WoT", C, D)]
WEIGHTS = BIASES + SETUP + IN_PR + IN_QKT + IN_UPT


def width(weights):
    return sum(c * n for _, c, n in weights)


ROWS = ["bv0", "b3", "bdown", "bo3"]

SCHEDULE = [
    ("A", "att_t"), ("B", "gcn_3a0"), ("C", "mha_xt"), ("B", "gcn_3a1"), ("C", "x2_bias"), ("B", "x1_stats"),
    ("B", "x1_norm"), ("A", "incidence"), ("C", "mha_qk"), ("A", "att_scores"), ("C", "mha_scores0"), ("A", "att_v"),
    ("C", "mha_max0"), ("A", "att_exp"), ("C", "mha_exp0a"), ("C", "mha_exp0b"), ("C", "mha_max1"), ("C", "mha_scores1"),
    ("C", "mha_v0"), ("C", "mha_v1"), ("A", "att_turn"), ("C", "mha_div0"), ("C", "mha_max2"), ("C", "mha_exp1a"),
    ("B", "hyper_x"), ("C", "mha_exp1b"), ("B", "x1_twice"), ("C", "mha_exp2a"), ("A", "att_out"), ("B", "hyper_rest"),
    ("A", "att_res1"), ("C", "mha_div1"), ("A", "x0_stats"), ("C", "mha_max3"), ("A", "x0_norm"), ("B", "hyper_up"),
    ("B", "up_out0"), ("B", "up_out1"), ("C", "mha_exp2b"), ("A", "gram"), ("A", "degrees"), ("C", "mha_turn0"),
    ("C", "mha_turn1"), ("A", "gram_scale"), ("A", "gcn_ax"), ("C", "mha_div2"), ("C", "mha_ctx0"),
    ("B", "up_high"), ("B", "up_rest0"), ("C", "mha_exp3a"), ("A", "gcn_1"), ("C", "mha_exp3b"), ("C", "mha_div3"),
    ("C", "mha_wo0"), ("C", "mha_turn2"), ("B", "up_rest1"), ("A", "gcn_2s0"), ("A", "gcn_2s1"), ("C", "mha_turn3"),
    ("B", "squares"), ("B", "square_sum"), ("A", "gcn_2a"), ("C", "mha_ctx1"), ("B", "hyper_down0"), ("A", "x0_bias"),
    ("A", "x_split"), ("C", "mha_wo1"), ("B", "hyper_y0"), ("C", "x3_stats0"), ("B", "hyper_down1"), ("B", "hyper_y1"),
    ("C", "x3_stats1"), ("A", "x_rest"),
    ("A", "gcn_3s0"), ("B", "hyper_out"), ("B", "x2_stats"), ("C", "x3_norm0"), ("B", "x2_norm"), ("C", "x3_norm1"),
    ("A", "gcn_3s1"), ("A", "gram_turn"),
]

DRAIN = [
    ("B", "gcn_3a0"), ("C", "mha_xt"), ("B", "gcn_3a1"), ("C", "mha_qk"), ("B", "x1_stats"), ("C", "x2_bias"),
    ("B", "x1_norm"), ("C", "mha_scores0"), ("C", "mha_v0"), ("C", "mha_v1"), ("C", "mha_max0"), ("C", "mha_exp0a"),
    ("C", "mha_exp0b"), ("C", "mha_max1"), ("C", "mha_scores1"), ("C", "mha_exp1a"), ("C", "mha_div0"), ("C", "mha_max2"),
    ("B", "hyper_x"), ("C", "mha_exp1b"), ("B", "hyper_rest"), ("C", "mha_max3"), ("C", "mha_div1"), ("C", "mha_exp2a"),
    ("B", "hyper_up"), ("B", "up_out0"), ("B", "up_out1"), ("B", "up_high"), ("B", "x1_twice"), ("C", "mha_exp2b"),
    ("C", "mha_turn0"), ("C", "mha_turn1"), ("C", "mha_div2"), ("B", "up_rest0"), ("C", "mha_exp3a"), ("C", "mha_ctx0"),
    ("C", "mha_exp3b"), ("C", "mha_wo0"), ("C", "mha_turn2"), ("C", "mha_div3"), ("B", "up_rest1"), ("C", "mha_turn3"),
    ("B", "squares"), ("B", "square_sum"), ("C", "x3_stats0"), ("C", "mha_ctx1"), ("C", "x3_norm0"), ("B", "hyper_down0"),
    ("C", "mha_wo1"), ("B", "hyper_y0"), ("B", "hyper_down1"), ("B", "hyper_y1"), ("B", "hyper_out"), ("B", "x2_stats"),
    ("C", "x3_stats1"), ("B", "x2_norm"), ("C", "x3_norm1"),
]

PARTED = ["att", "Wv0T", "W1", "W2", "W3", "WupT", "WdownT", "Wqk3T", "Wv3T", "WoT"]


def build(nc, A):
    NG = A["x"].shape[0]

    ctx = ExitStack()
    with ctx:
        def sb(name, shape, dtype=F32):
            return ctx.enter_context(nc.sbuf_tensor(name, shape, dtype))

        def sem(name):
            return ctx.enter_context(nc.semaphore(name))

        ps = ctx.enter_context(nc.psum_tensor("ps", [P, 8, 512], F32))
        ps4 = ps[:].rearrange("p k (b n) -> p k b n", b=GB)
        ps2 = ps[:].rearrange("p k (b n) -> p k b n", b=2)

        pr = sb("pr", [P, GB, HEADS, P]); prT = sb("prT", [P, 2, HEADS, P])
        qkT = sb("qkT", [P, 2 * C, N4]); upT = sb("upT", [P, HC, N4])
        pr_flat = pr[:].rearrange("p b h n -> p (b h n)")
        qkT_flat = qkT[:].rearrange("p c n -> p (c n)"); upT_flat = upT[:].rearrange("p c n -> p (c n)")

        biases = sb("biases", [P, width(BIASES)])
        w = {}
        for place, names in ((biases[:], BIASES), (pr_flat, SETUP + IN_PR), (qkT_flat, IN_QKT),
                             (upT_flat, IN_UPT + [("att", C, D)])):
            at = 0
            for name, chunks, cols in names:
                w[name] = place[:, at:at + chunks * cols].rearrange("p (c n) -> p c n", c=chunks)
                at += chunks * cols
        wq0, wk0, w_down, w_o = w["Wq0"], w["Wk0"], w["WdownT"], w["WoT"]
        bq0, bk0, b_g1, b_g2, b_up = w["bq0"], w["bk0"], w["b1"], w["b2"], w["bup"]
        gam, bet, b_qk = w["gamma"], w["beta"], w["bqk3"]
        high = {name: sb(f"{name}_high", list(w[name].shape), F32R) for name in PARTED}
        rest = {name: sb(f"{name}_rest", list(w[name].shape), F32R) for name in PARTED}
        t0 = sb("t0", [P, C])
        rows = sb("rows", [P, len(ROWS), D])
        r_v0, r_g3, r_b2, r_o = (rows[:, i] for i in range(len(ROWS)))
        c0 = sb("c0", [P, 1])
        r_down = sb("r_down", [P, D])
        ident = sb("ident", [P, P]); ones = sb("ones", [P, P])
        mean_mat = sb("mean_mat", [P, P])

        x = sb("x", [P, GB, D]); xT = sb("xT", [P, C, N4])
        adjA = sb("adjA", [P, GB, P]); adjTA = sb("adjTA", [P, GB, P])
        tT = sb("tT", [P, C, N4])
        z1T = z2T = tT
        s2 = s3 = sb("s2_s3", [P, GB, D])
        x2T = gxT = axT = z_high = sb("fT_high", [P, C, N4], F32R)
        fT_rest = sb("fT_rest", [P, C, N4], F32R)
        xT_high = sb("xT_high", [P, C, N4], F32R); xT_rest = sb("xT_rest", [P, C, N4], F32R)
        v0 = sb("v0", [P, GB, D + 1])
        off0 = sb("off0", [P, GB]); raw0 = sb("raw0", [P, GB])
        e0 = sb("e0", [P, GB, P]); p0 = sb("p0", [P, GB, P])
        p0T = sb("p0T", [P, N4]); rs0 = sb("rs0", [P, GB]); x0 = sb("x0", [P, GB, D])
        x1 = sb("x1", [P, GB, D])
        hT = sb("hT", [P, GB, P]); cnt = sb("cnt", [P, 3, GB]); bhT = sb("bhT", [P, GB, P + 1])
        dn = sb("dn", [P, 5, GB]); gm = sb("gm", [P, GB, P]); gmT = sb("gmT", [P, GB, P])
        up_high = sb("up_high", [P, HC, N4], F32R); up_rest = sb("up_rest", [P, HC, N4], F32R)
        sqs = sb("sqs", [P, 2, N4])
        mom = sb("mom", [P, GB, 2]); hv = sb("hv", [P, 4, GB]); y2 = sb("y2", [P, GB, D])
        x2 = sb("x2", [P, GB, D])
        adjB = sb("adjB", [P, GB, P]); v3 = sb("v3", [P, GB, D])
        mx = sb("mx", [P, GB, 2, HEADS]); den = sb("den", [P, GB, 2, HEADS])
        ctxT = sb("ctxT", [P, C, 2, P], F32R); ctx_rest = sb("ctx_rest", [P, C, 2, P], F32R)
        x3 = sb("x3", [P, GB, D])
        rep = prT[:].rearrange("p t h n -> p (t h) n")
        st = [sb(f"st{i}", [P, GB, 6]) for i in range(4)]
        mv = [sb(f"mv{i}", [P, GB, 2]) for i in range(4)]
        var = [sb(f"var{i}", [P, GB]) for i in range(4)]
        rstd = [sb(f"rstd{i}", [P, GB]) for i in range(4)]
        held = sb("held", [P, 1])
        neg_half = sb("neg_half", [P, GB])

        setup_in = sem("setup_in"); weights_in = sem("weights_in"); ident_ready = sem("ident_ready")
        setup_done = sem("setup_done")
        ones_ready = sem("ones_ready"); setup_mm = sem("setup_mm"); consts_ready = sem("consts_ready")
        parts_high = sem("parts_high"); att_ready = sem("att_ready"); parts_ready = sem("parts_ready")
        x_high_ready = sem("x_high_ready"); x_rest_ready = sem("x_rest_ready")
        ax_rest = sem("ax_rest"); z1_full = sem("z1_full"); z1_rest = sem("z1_rest")
        z2_full = sem("z2_full"); z2_rest = sem("z2_rest")
        up_high_ready = sem("up_high_ready"); up_rest_ready = sem("up_rest_ready"); ctx_rest_ready = sem("ctx_rest_ready")
        gx_rest = sem("gx_rest"); x2T_rest = sem("x2T_rest")
        x_in = sem("x_in"); xT_in = sem("xT_in"); adjA_in = sem("adjA_in"); adjTA_in = sem("adjTA_in")
        adjB_in = sem("adjB_in"); out_stored = sem("out_stored")
        t_done = sem("t_done"); t_ready = sem("t_ready"); v0_done = sem("v0_done"); v0_ready = sem("v0_ready")
        s0_done = sem("s0_done"); e0_ready = sem("e0_ready"); p0_ready = sem("p0_ready")
        p0T_done = sem("p0T_done"); p0T_ready = sem("p0T_ready"); att_done = sem("att_done")
        rs0_ready = sem("rs0_ready"); off0_ready = sem("off0_ready"); xb_ready = sem("xb_ready"); res0_ready = sem("res0_ready")
        norm_step = [sem(f"norm{i}_step") for i in range(4)]
        rstd_ready = [sem(f"rstd{i}_ready") for i in range(4)]
        x0_ready = sem("x0_ready"); ax_done = sem("ax_done"); ax_ready = sem("ax_ready")
        z1_done = sem("z1_done"); z1_ready = sem("z1_ready"); s2_done = sem("s2_done"); s2_ready = sem("s2_ready")
        z2_done = sem("z2_done"); z2_ready = sem("z2_ready"); s3_done = sem("s3_done"); s3_ready = sem("s3_ready")
        x0b_ready = sem("x0b_ready"); gcn_done = sem("gcn_done"); res1_ready = sem("res1_ready"); x1_ready = sem("x1_ready")
        inc_step = sem("inc_step"); inc_ready = sem("inc_ready"); gram_done = sem("gram_done")
        degree_step = sem("degree_step"); gm_ready = sem("gm_ready"); gmT_done = sem("gmT_done"); gmT_ready = sem("gmT_ready")
        gx_done = sem("gx_done"); gx_ready = sem("gx_ready"); up_done = sem("up_done"); up_ready = sem("up_ready")
        sq_ready = sem("sq_ready"); sqs_step = sem("sqs_step"); sqs_ready = sem("sqs_ready")
        down_done = sem("down_done"); var_step = sem("var_step"); h_rstd_ready = sem("h_rstd_ready"); y2_ready = sem("y2_ready")
        x1d_step = sem("x1d_step"); x1d_ready = sem("x1d_ready"); hyper_done = sem("hyper_done")
        res2_ready = sem("res2_ready"); x2_ready = sem("x2_ready"); x2T_done = sem("x2T_done"); x2T_ready = sem("x2T_ready")
        qk_done = sem("qk_done"); qk_ready = sem("qk_ready"); v3_done = sem("v3_done"); v3_ready = sem("v3_ready")
        s3h_done = sem("mha_scores_done"); masked_ready = sem("masked_ready"); mx_step = sem("mx_step")
        mx_ready = sem("mx_ready"); exp_ready = sem("exp_ready"); den_step = sem("den_step"); pr_ready = sem("pr_ready")
        prT_done = sem("prT_done"); prT_act = sem("prT_even_ready"); prT_dve = sem("prT_odd_ready")
        ctx_done = sem("ctx_done"); ctx_ready = sem("ctx_ready"); x2b_ready = sem("x2b_ready")
        wo_done = sem("wo_done"); res3_ready = sem("res3_ready"); x3_ready = sem("x3_ready")

        block = ctx.enter_context(nc.Block())

        def run(eng, steps, last_in_loop=NG - 1):
            def turn(t):
                order = DRAIN if isinstance(t, int) and t >= NG else SCHEDULE
                for stage, name in order:
                    back = "ABC".index(stage)
                    if name in steps and not (isinstance(t, int) and not 0 <= t - back < NG):
                        steps[name](t - back)
            for t in range(3):
                turn(t)
            with eng.Fori(3, last_in_loop + 1) as t:
                turn(t)
            for t in range(last_in_loop + 1, NG + 2):
                turn(t)

        def ahead(n, k, g):
            return n * (min(g + k, NG - 1) + 1) if isinstance(g, int) else n * (g + k + 1)

        def att_bank(b):
            return (b + 2) % 4

        def turn_bank(b):
            return 4 if b in (0, 3) else 6

        def first(g):
            return isinstance(g, int) and g == 0

        def final(g):
            return isinstance(g, int) and g == NG - 1

        @block.sync
        def _(sp):
            at = [width(WEIGHTS[:n]) for n in range(len(WEIGHTS) + 1)]
            n_b, n_s, n_p, n_q = len(BIASES), len(SETUP), len(IN_PR), len(IN_QKT)
            sp.dma_start(biases[:], A["weights"][:, 0:at[n_b]]).then_inc(setup_in, 16)
            sp.dma_start(pr_flat[:, 0:width(SETUP)], A["weights"][:, at[n_b]:at[n_b + n_s]]).then_inc(setup_in, 16)
            sp.dma_start(rows[:], A["rows"].partition_broadcast(P)).then_inc(setup_in, 16)
            sp.dma_start(xT[:], A["xT"][0]).then_inc(xT_in, 16)
            sp.dma_start(adjA[:], A["adj"][0]).then_inc(adjA_in, 16)
            sp.dma_start(x[:], A["x"][0]).then_inc(x_in, 16)
            sp.dma_start(adjTA[:], A["adjT"][0]).then_inc(adjTA_in, 16)
            sp.dma_start(upT_flat[:, 0:width(IN_UPT)],
                         A["weights"][:, at[n_b + n_s + n_p + n_q]:at[-1]]).then_inc(weights_in, 16)
            sp.dma_start(pr_flat[:, width(SETUP):width(SETUP + IN_PR)],
                         A["weights"][:, at[n_b + n_s]:at[n_b + n_s + n_p]]).then_inc(weights_in, 16)
            sp.dma_start(qkT_flat, A["weights"][:, at[n_b + n_s + n_p]:at[n_b + n_s + n_p + n_q]]).then_inc(weights_in, 16)
            sp.dma_start(adjB[:], A["adj"][0]).then_inc(adjB_in, 16)

            def next_xT(g):
                if not final(g):
                    sp.wait_ge(s0_done, g + 1)
                    sp.dma_start(xT[:], A["xT"][g + 1]).then_inc(xT_in, 16)

            def next_adjA(g):
                if not final(g):
                    sp.wait_ge(p0_ready, GB * g + GB)
                    sp.dma_start(adjA[:], A["adj"][g + 1]).then_inc(adjA_in, 16)

            def next_x(g):
                if not final(g):
                    sp.wait_ge(res0_ready, GB * g + GB)
                    sp.dma_start(x[:], A["x"][g + 1]).then_inc(x_in, 16)

            def next_adjTA(g):
                if not final(g):
                    sp.wait_ge(gcn_done, 2 * g + 2)
                    sp.wait_ge(inc_ready, g + 1)
                    sp.dma_start(adjTA[:], A["adjT"][g + 1]).then_inc(adjTA_in, 16)

            def next_adjB(g):
                if not final(g):
                    sp.wait_ge(masked_ready, GB * g + GB)
                    sp.dma_start(adjB[:], A["adj"][g + 1]).then_inc(adjB_in, 16)

            def store(g):
                sp.wait_ge(x3_ready, GB * g + GB)
                sp.dma_start(A["out"][g], x3[:]).then_inc(out_stored, 16)

            run(sp, {"att_scores": next_xT, "att_turn": next_adjA, "att_out": next_x, "gcn_3a1": next_adjTA,
                     "mha_scores1": next_adjB, "x3_norm1": store}, NG - 2)
            sp.wait_ge(out_stored, 16 * NG)

        @block.tensor
        def _(pe):
            def mm(out, lhsT, rhs, k=0, n=1):
                return pe.matmul(out, lhsT, rhs, start=(k == 0), stop=(k == n - 1))

            def high_passes(out, weight, cols, data, c):
                mm(out, high[weight][:, c, cols], data[:, c, :], 2 * c, 3 * C)
                mm(out, rest[weight][:, c, cols], data[:, c, :], 2 * c + 1, 3 * C)

            def rest_pass(out, weight, cols, data_rest, c):
                return mm(out, high[weight][:, c, cols], data_rest[:, c, :], 2 * C + c, 3 * C)

            def high_rows(out, weight, data, n, chunks=C):
                for c in range(chunks):
                    mm(out, data[:, c, n], high[weight][:, c, :], 2 * c, 3 * chunks)
                    mm(out, data[:, c, n], rest[weight][:, c, :], 2 * c + 1, 3 * chunks)

            def rest_rows(out, weight, data_rest, n, chunks=C):
                for c in range(chunks):
                    last = mm(out, data_rest[:, c, n], high[weight][:, c, :], 2 * chunks + c, 3 * chunks)
                return last

            def graph(b):
                return slice(b * P, (b + 1) * P)

            pe.wait_ge(consts_ready, 1)
            for m in range(C):
                for o in range(C):
                    mm(ps[:, m, 0:D], wq0[:, o, m * P:(m + 1) * P], wk0[:, o, :], o, C)
                for o in range(C):
                    mm(ps[:, m, D:D + 1], wk0[:, o, m * P:(m + 1) * P], bq0[:, o, :], o, C)
                for o in range(C):
                    mm(ps[:, m, D + 1:D + 2], wq0[:, o, m * P:(m + 1) * P], bk0[:, o, :], o, C)
            for o in range(C):
                last = mm(ps[:, 2, 0:1], rep[:, o, :], bk0[:, o, :], o, C)
            last.then_inc(setup_mm, 1)
            for f in range(HC):
                mm(ps[:, 3, 0:D], rep[:, C + f, :], w_down[:, f, 0:D], f, HC)
            for f in range(HC):
                last = mm(ps[:, 4, 0:D], rep[:, 2 * C + HC + f, :], w_down[:, f, 0:D], f, HC)
            last.then_inc(setup_mm, 1)
            pe.wait_ge(weights_in, 48)
            for o in range(C):
                last = mm(ps[:, 5, 0:D], rep[:, C + HC + o, :], w_o[:, o, :], o, C)
            last.then_inc(setup_mm, 1)
            pe.wait_ge(ident_ready, 2)
            pe.wait_ge(setup_done, 1)

            def att_t(g):
                if first(g):
                    pe.wait_ge(parts_ready, 2)
                pe.wait_ge(x_high_ready, g + 1)
                for m in range(C):
                    if m == 1 and not first(g):
                        pe.wait_ge(gmT_ready, g)
                    for c in range(C):
                        high_passes(ps[:, 1 - m, :], "att", slice(m * P, (m + 1) * P), xT_high, c)
                pe.wait_ge(x_rest_ready, g + 1)
                for m in range(C):
                    for c in range(C):
                        last = rest_pass(ps[:, 1 - m, :], "att", slice(m * P, (m + 1) * P), xT_rest, c)
                    last.then_inc(t_done, 1)

            def att_v(g):
                for b in range(GB):
                    if b < 2:
                        if not first(g):
                            pe.wait_ge(res1_ready, 2 * g)
                    else:
                        pe.wait_ge(v0_ready, GB * g + b - 1)
                    high_rows(ps[:, 2 + b % 2, 0:D + 2], "Wv0T", xT_high, graph(b))
                    rest_rows(ps[:, 2 + b % 2, 0:D + 2], "Wv0T", xT_rest, graph(b)).then_inc(v0_done, 1)

            def att_scores(g):
                pe.wait_ge(t_ready, 2 * g + 2)
                for b in range(GB):
                    for c in range(C):
                        last = mm(ps4[:, 0, b], tT[:, c, b * P:(b + 1) * P], xT[:, c, b * P:(b + 1) * P], c, C)
                last.then_inc(s0_done, 1)

            def att_turn(g):
                for b in range(GB):
                    pe.wait_ge(p0_ready, GB * g + b + 1)
                    last = pe.transpose(ps4[:, 1, b], p0[:, b, :], ident[:])
                last.then_inc(p0T_done, 1)

            def att_out(g):
                pe.wait_ge(v0_ready, GB * g + GB)
                pe.wait_ge(p0T_ready, g + 1)
                for b in range(GB):
                    if b < 2 and not (isinstance(g, int) and g < 2):
                        pe.wait_ge(v3_ready, 2 * g - 3 + b)
                    mm(ps[:, att_bank(b), 0:D + 1], p0T[:, b * P:(b + 1) * P], v0[:, b, 0:D + 1]).then_inc(att_done, 1)

            def gcn_ax(g):
                pe.wait_ge(adjTA_in, 16 * g + 16)
                for b in range(GB):
                    pe.wait_ge(x0_ready, GB * g + b + 1)
                    for c in range(C):
                        last = mm(ps4[:, 2 + c, b], x0[:, b, c * P:(c + 1) * P], adjTA[:, b, :])
                last.then_inc(ax_done, 1)

            def gcn_1(g):
                if first(g):
                    pe.wait_ge(parts_ready, 5)
                pe.wait_ge(gm_ready, 2 * g + 2)
                for m in range(C):
                    for c in range(C):
                        pe.wait_ge(ax_ready, 2 * g + c + 1)
                        high_passes(ps[:, m, :], "W1", slice(m * P, (m + 1) * P), axT, c)
                pe.wait_ge(ax_rest, 2 * g + 2)
                for m in range(C):
                    for c in range(C):
                        last = rest_pass(ps[:, m, :], "W1", slice(m * P, (m + 1) * P), fT_rest, c)
                    last.then_inc(z1_done, 1)

            def gcn_2s(g, pair):
                pe.wait_ge(z1_ready, 2 * g + 2)
                for b in (2 * pair, 2 * pair + 1):
                    high_rows(ps2[:, 2 + pair, b % 2], "W2", z_high, graph(b))
                    pe.wait_ge(z1_rest, g + 1)
                    last = rest_rows(ps2[:, 2 + pair, b % 2], "W2", fT_rest, graph(b))
                last.then_inc(s2_done, 1)

            def gcn_2a(g):
                for b in range(GB):
                    pe.wait_ge(s2_ready, 2 * g + 1 + b // 2)
                    for m in range(C):
                        last = mm(ps4[:, m, b], s2[:, b, m * P:(m + 1) * P], adjTA[:, b, :])
                last.then_inc(z2_done, 1)

            def gcn_3s(g, pair):
                pe.wait_ge(z2_ready, 2 * g + 2)
                for b in (2 * pair, 2 * pair + 1):
                    high_rows(ps2[:, 2 + pair, b % 2], "W3", z_high, graph(b))
                    pe.wait_ge(z2_rest, g + 1)
                    last = rest_rows(ps2[:, 2 + pair, b % 2], "W3", fT_rest, graph(b))
                last.then_inc(s3_done, 1)

            def gcn_3a(g, pair):
                pe.wait_ge(s3_ready, 2 * g + 1 + pair)
                for b in (2 * pair, 2 * pair + 1):
                    last = mm(ps2[:, 2 + pair, b % 2], adjTA[:, b, :], s3[:, b, :])
                last.then_inc(gcn_done, 1)

            def gram(g):
                pe.wait_ge(inc_ready, g + 1)
                pe.wait_ge(res0_ready, GB * g + GB)
                for b in range(GB):
                    last = mm(ps[:, b // 2, (b % 2) * (P + 1):(b % 2 + 1) * (P + 1)], hT[:, b, :], bhT[:, b, :])
                last.then_inc(gram_done, 1)

            def gram_turn(g):
                for b in range(GB):
                    pe.wait_ge(gm_ready, 2 * g + 1 + b // 2)
                    last = pe.transpose(ps4[:, 0, b], gm[:, b, :], ident[:])
                last.then_inc(gmT_done, 1)

            def hyper_x(g):
                if not first(g):
                    pe.wait_ge(masked_ready, GB * g)
                for b in range(GB):
                    pe.wait_ge(x1_ready, GB * g + b + 1)
                    for c in range(C):
                        last = mm(ps4[:, 6 + c, b], x1[:, b, c * P:(c + 1) * P], gmT[:, b, :])
                last.then_inc(gx_done, 1)

            def hyper_up(g):
                def high_part(m):
                    for c in range(C):
                        pe.wait_ge(gx_ready, 2 * g + c + 1)
                        high_passes(ps[:, 4 + m, :], "WupT", slice(m * P, (m + 1) * P), gxT, c)

                def rest_part(m):
                    for c in range(C):
                        last = rest_pass(ps[:, 4 + m, :], "WupT", slice(m * P, (m + 1) * P), fT_rest, c)
                    last.then_inc(up_done, 1)

                if first(g):
                    pe.wait_ge(parts_ready, len(PARTED))
                high_part(0)
                high_part(1)
                pe.wait_ge(gx_rest, 2 * g + 2)
                rest_part(0)
                rest_part(1)
                for m in (2, 3):
                    high_part(m)
                    rest_part(m)

            def hyper_down(g, half):
                pe.wait_ge(up_high_ready, g + 1)
                pe.wait_ge(up_rest_ready, 2 * g + 2)
                for b in (2 * half, 2 * half + 1):
                    if b == 3 and not first(g):
                        pe.wait_ge(res3_ready, 2 * g)
                    high_rows(ps[:, 4 + b, 0:D + 2], "WdownT", up_high, graph(b), HC)
                    rest_rows(ps[:, 4 + b, 0:D + 2], "WdownT", up_rest, graph(b), HC)
                pe.wait_ge(sqs_ready, g + 1)
                for b in (2 * half, 2 * half + 1):
                    mm(ps[:, 4 + b, D + 1:D + 2], sqs[:, 0, b * P:(b + 1) * P], mean_mat[:, 0:1]).then_inc(down_done, 1)

            def hyper_out(g):
                for b in range(GB):
                    pe.wait_ge(y2_ready, GB * g + b + 1)
                    last = mm(ps2[:, 4 + b // 2, b % 2], gmT[:, b, :], y2[:, b, :])
                    if b % 2:
                        last.then_inc(hyper_done, 1)

            def mha_xt(g):
                for b in range(GB):
                    pe.wait_ge(x2_ready, GB * g + b + 1)
                    for c in range(C):
                        last = pe.transpose(ps4[:, 6 + c, b], x2[:, b, c * P:(c + 1) * P], ident[:])
                last.then_inc(x2T_done, 1)

            def mha_qk(g):
                def high_part(m):
                    for c in range(C):
                        pe.wait_ge(x2T_ready, 2 * g + c + 1)
                        high_passes(ps[:, 4 + m, :], "Wqk3T", slice(m * P, (m + 1) * P), x2T, c)

                def rest_part(m):
                    for c in range(C):
                        last = rest_pass(ps[:, 4 + m, :], "Wqk3T", slice(m * P, (m + 1) * P), fT_rest, c)
                    last.then_inc(qk_done, 1)

                high_part(0)
                high_part(1)
                pe.wait_ge(x2T_rest, 2 * g + 2)
                rest_part(0)
                rest_part(1)
                for m in (2, 3):
                    high_part(m)
                    rest_part(m)

            def mha_v(g, pair):
                if pair == 0:
                    pe.wait_ge(res1_ready, ahead(2, 1, g))
                    pe.wait_ge(v0_ready, ahead(GB, 2, g))
                for b in (2 * pair, 2 * pair + 1):
                    high_rows(ps2[:, 2 + pair, b % 2], "Wv3T", x2T, graph(b))
                    last = rest_rows(ps2[:, 2 + pair, b % 2], "Wv3T", fT_rest, graph(b))
                last.then_inc(v3_done, 1)

            def mha_scores(g, pair):
                if pair == 0:
                    pe.wait_ge(qk_ready, 4 * g + 4)
                else:
                    pe.wait_ge(masked_ready, GB * g + 2)
                for bb in range(2):
                    b = 2 * pair + bb
                    for i in range(C):
                        for j in range(JR):
                            rows = slice(j * DH, (j + 1) * DH)
                            last = mm(ps4[:, 4 + j, 2 * bb + i], qkT[rows, i, graph(b)], qkT[rows, C + i, graph(b)])
                last.then_inc(s3h_done, 1)

            def mha_turn(g, b):
                pe.wait_ge(pr_ready, GB * g + b + 1)
                if b < 2:
                    pe.wait_ge(up_ready, ahead(4, 1, g) - 2 + 2 * b)
                if b == 3:
                    pe.wait_ge(res3_ready, 2 * g + 1)
                for k in range(HEADS):
                    last = pe.transpose(ps4[:, turn_bank(b) + k // 4, k % 4], pr[:, b, k, :], ident[:])
                last.then_inc(prT_done, 1)

            def mha_ctx(g, pair):
                pe.wait_ge(v3_ready, 2 * g + pair + 1)
                pe.wait_ge(prT_act, GB * g + 2 * pair + 2)
                pe.wait_ge(prT_dve, GB * g + 2 * pair + 2)
                for bb in range(2):
                    b = 2 * pair + bb
                    for i in range(C):
                        for j in range(JR):
                            h = JR * i + j
                            last = mm(ps4[j * DH:(j + 1) * DH, 4 + 2 * pair, 2 * i + bb], v3[:, b, h * DH:(h + 1) * DH],
                                      prT[:, bb, 2 * j + i, :])
                last.then_inc(ctx_done, 1)

            def mha_wo(g, pair):
                pe.wait_ge(ctx_ready, 2 * g + pair + 1)
                for bb in range(2):
                    high_rows(ps2[:, 5 + 2 * pair, bb], "WoT", ctxT[:, :, bb, :], slice(0, P))
                    pe.wait_ge(ctx_rest_ready, 2 * g + pair + 1)
                    last = rest_rows(ps2[:, 5 + 2 * pair, bb], "WoT", ctx_rest[:, :, bb, :], slice(0, P))
                last.then_inc(wo_done, 1)

            run(pe, {
                "att_t": att_t, "att_v": att_v, "att_scores": att_scores, "att_turn": att_turn, "att_out": att_out,
                "gcn_ax": gcn_ax, "gram": gram, "gcn_1": gcn_1, "gram_turn": gram_turn, "gcn_2a": gcn_2a,
                "gcn_2s0": lambda g: gcn_2s(g, 0), "gcn_2s1": lambda g: gcn_2s(g, 1),
                "gcn_3s0": lambda g: gcn_3s(g, 0), "gcn_3s1": lambda g: gcn_3s(g, 1),
                "gcn_3a0": lambda g: gcn_3a(g, 0), "gcn_3a1": lambda g: gcn_3a(g, 1), "hyper_x": hyper_x,
                "hyper_up": hyper_up, "hyper_down0": lambda g: hyper_down(g, 0),
                "hyper_down1": lambda g: hyper_down(g, 1), "hyper_out": hyper_out, "mha_xt": mha_xt,
                "mha_qk": mha_qk, "mha_v0": lambda g: mha_v(g, 0), "mha_v1": lambda g: mha_v(g, 1),
                "mha_scores0": lambda g: mha_scores(g, 0), "mha_scores1": lambda g: mha_scores(g, 1),
                "mha_turn0": lambda g: mha_turn(g, 0), "mha_turn1": lambda g: mha_turn(g, 1),
                "mha_turn2": lambda g: mha_turn(g, 2), "mha_turn3": lambda g: mha_turn(g, 3),
                "mha_ctx0": lambda g: mha_ctx(g, 0), "mha_ctx1": lambda g: mha_ctx(g, 1),
                "mha_wo0": lambda g: mha_wo(g, 0), "mha_wo1": lambda g: mha_wo(g, 1)})

        @block.scalar
        def _(act):
            def att_t(g):
                for m in range(C):
                    act.wait_ge(t_done, 2 * g + m + 1)
                    act.activation(tT[:, m, :], ps[:, 1 - m, :], ACT.Identity, bias=t0[:, m:m + 1]).then_inc(t_ready, 1)

            def att_v(g):
                for b in range(GB):
                    act.wait_ge(v0_done, GB * g + b + 1)
                    act.copy(raw0[:, b:b + 1], ps[:, 2 + b % 2, D:D + 1])
                    act.copy(v0[:, b, 0:D], ps[:, 2 + b % 2, 0:D]).then_inc(v0_ready, 1)
                act.wait_ge(v0_ready, GB * g + GB)
                act.activation(off0[:], raw0[:], ACT.Identity, bias=c0[:]).then_inc(off0_ready, 1)

            def att_exp(g):
                act.wait_ge(s0_done, g + 1)
                act.wait_ge(off0_ready, g + 1)
                for b in range(GB):
                    act.activation(e0[:, b, :], ps4[:, 0, b], ACT.Exp, bias=off0[:, b:b + 1]).then_inc(e0_ready, 1)

            def att_turn(g):
                act.wait_ge(p0T_done, g + 1)
                act.copy(p0T[:], ps[:, 1, :]).then_inc(p0T_ready, 1)

            def mha_v(g, k):
                act.wait_ge(v3_done, 2 * g + k + 1)
                act.copy(v3[:, 2 * k:2 * k + 2, :], ps2[:, 2 + k]).then_inc(v3_ready, 1)

            def gcn_ax(g):
                act.wait_ge(ax_done, g + 1)
                for c in range(C):
                    act.copy(axT[:, c, :], ps[:, 2 + c, :]).then_inc(ax_ready, 1)

            def gcn_1(g):
                for m in range(C):
                    act.wait_ge(z1_done, 2 * g + m + 1)
                    act.activation(z1T[:, m, :], ps[:, m, :], ACT.Relu, bias=b_g1[:, m, :]).then_inc(z1_full, 1)

            def gcn_2s(g, k):
                act.wait_ge(s2_done, 2 * g + k + 1)
                act.copy(s2[:, 2 * k:2 * k + 2, :], ps2[:, 2 + k]).then_inc(s2_ready, 1)

            def gcn_2a(g):
                act.wait_ge(z2_done, g + 1)
                for m in range(C):
                    act.activation(z2T[:, m, :], ps[:, m, :], ACT.Relu, bias=b_g2[:, m, :]).then_inc(z2_full, 1)

            def gcn_3s(g, k):
                act.wait_ge(s3_done, 2 * g + k + 1)
                act.copy(s3[:, 2 * k:2 * k + 2, :], ps2[:, 2 + k]).then_inc(s3_ready, 1)

            def x_high(g):
                act.wait_ge(xT_in, 16 * g + 16)
                act.copy(xT_high[:], xT[:]).then_inc(x_high_ready, 1)

            def x_split(g):
                if not final(g):
                    x_high(g + 1)

            def gram_turn(g):
                act.wait_ge(gmT_done, g + 1)
                if not first(g):
                    act.wait_ge(hyper_done, 2 * g)
                act.copy(gmT[:], ps4[:, 0]).then_inc(gmT_ready, 1)

            def hyper_x(g):
                act.wait_ge(gx_done, g + 1)
                for c in range(C):
                    act.copy(gxT[:, c, :], ps[:, 6 + c, :]).then_inc(gx_ready, 1)

            def up_out(g, half):
                if not first(g):
                    act.wait_ge(sqs_ready, g)
                for f in (2 * half, 2 * half + 1):
                    act.wait_ge(up_done, 4 * g + f + 1)
                    act.activation(upT[:, f, :], ps[:, 4 + f, :], ACT.Relu, bias=b_up[:, f, :]).then_inc(up_ready, 1)

            def squares(g):
                for f in range(HC):
                    act.wait_ge(up_rest_ready, 2 * g + 1 + f // 2)
                    act.activation(upT[:, f, :], upT[:, f, :], ACT.Square).then_inc(sq_ready, 1)

            def mha_xt(g):
                act.wait_ge(x2T_done, g + 1)
                for c in range(C):
                    act.copy(x2T[:, c, :], ps[:, 6 + c, :]).then_inc(x2T_ready, 1)

            def mha_qk(g):
                for m in range(2 * C):
                    act.wait_ge(qk_done, 4 * g + m + 1)
                    act.activation(qkT[:, m, :], ps[:, 4 + m, :], ACT.Identity, bias=b_qk[:, m, :]).then_inc(qk_ready, 1)

            def mha_exp(g, b, half):
                act.wait_ge(mx_ready, GB * g + b + 1)
                for k in range(half * HEADS // 2, (half + 1) * HEADS // 2):
                    act.activation(pr[:, b, k, :], pr[:, b, k, :], ACT.Exp, bias=mx[:, b, 1, k:k + 1], scale=ATT,
                                   accum_out=den[:, b, 0, k:k + 1]).then_inc(exp_ready, 1)

            def mha_turn(g, b):
                act.wait_ge(prT_done, GB * g + b + 1)
                act.copy(prT[:, b % 2, 0:4, :], ps4[:, turn_bank(b)]).then_inc(prT_act, 1)

            def mha_ctx(g, pair):
                act.wait_ge(ctx_done, 2 * g + pair + 1)
                act.copy(ctxT[:].rearrange("p i b n -> p (i b) n"), ps4[:, 4 + 2 * pair]).then_inc(ctx_ready, 1)

            x_high(0)
            for name in PARTED:
                if name == "att":
                    act.wait_ge(att_ready, 1)
                if name == "W1":
                    act.wait_ge(weights_in, 48)
                if name == "WdownT":
                    act.wait_ge(setup_done, 1)
                act.copy(high[name][:], w[name][:]).then_inc(parts_high, 1)
            run(act, {
                "att_t": att_t, "att_v": att_v, "att_exp": att_exp, "att_turn": att_turn, "gcn_ax": gcn_ax,
                "gcn_1": gcn_1, "mha_v0": lambda g: mha_v(g, 0), "mha_v1": lambda g: mha_v(g, 1),
                "gram_turn": gram_turn, "gcn_2a": gcn_2a, "x_split": x_split, "gcn_3s0": lambda g: gcn_3s(g, 0),
                "gcn_3s1": lambda g: gcn_3s(g, 1), "gcn_2s0": lambda g: gcn_2s(g, 0),
                "gcn_2s1": lambda g: gcn_2s(g, 1), "squares": squares, "hyper_x": hyper_x,
                "up_out0": lambda g: up_out(g, 0), "up_out1": lambda g: up_out(g, 1), "mha_xt": mha_xt,
                "mha_qk": mha_qk, "mha_exp0a": lambda g: mha_exp(g, 0, 0), "mha_exp0b": lambda g: mha_exp(g, 0, 1),
                "mha_exp1a": lambda g: mha_exp(g, 1, 0), "mha_exp1b": lambda g: mha_exp(g, 1, 1),
                "mha_exp2a": lambda g: mha_exp(g, 2, 0), "mha_exp2b": lambda g: mha_exp(g, 2, 1),
                "mha_exp3a": lambda g: mha_exp(g, 3, 0), "mha_exp3b": lambda g: mha_exp(g, 3, 1),
                "mha_turn0": lambda g: mha_turn(g, 0), "mha_turn1": lambda g: mha_turn(g, 1),
                "mha_turn2": lambda g: mha_turn(g, 2), "mha_turn3": lambda g: mha_turn(g, 3),
                "mha_ctx0": lambda g: mha_ctx(g, 0), "mha_ctx1": lambda g: mha_ctx(g, 1)}, NG - 2)

        @block.vector
        def _(dve):
            dve.memset(ones[:], 1.0)
            dve.memset(mean_mat[:], 1.0 / HID)
            dve.memset(v0[:, :, D:D + 1], 1.0).then_inc(ones_ready, 1)
            dve.wait_ge(ones_ready, 1)
            dve.wait_ge(setup_in, 48)
            for c in range(C):
                dve.tensor_scalar(rep[:, c, :], ones[:], bq0[:, c, :], None, ALU.mult)
            for f in range(HC):
                dve.tensor_scalar(rep[:, C + f, :], ones[:], bet[:, f, :], None, ALU.mult)
                dve.tensor_scalar(rep[:, 2 * C + HC + f, :], mean_mat[:], gam[:, f, :], None, ALU.mult)
            for c in range(C):
                last = dve.tensor_scalar(rep[:, C + HC + c, :], ones[:], w["bv3"][:, c, :], None, ALU.mult)
            last.then_inc(consts_ready, 1)

            def make_rest(name):
                dve.wait_ge(parts_high, PARTED.index(name) + 1)
                dve.tensor_tensor(rest[name][:], w[name][:], high[name][:], ALU.subtract).then_inc(parts_ready, 1)

            dve.wait_ge(setup_mm, 1)
            for m in range(C):
                dve.tensor_copy(w["att"][:, m, :], ps[:, m, 0:D])
                dve.tensor_copy(t0[:, m:m + 1], ps[:, m, D:D + 1])
                last = dve.tensor_copy(w["Wv0T"][:, m, D:D + 1], ps[:, m, D + 1:D + 2])
            last.then_inc(att_ready, 1)
            dve.tensor_copy(c0[:], ps[:, 2, 0:1])
            make_rest("att")
            make_rest("Wv0T")
            dve.wait_ge(setup_mm, 2)
            dve.tensor_copy(r_down[:], ps[:, 3, 0:D])
            for f in range(HC):
                dve.scalar_tensor_tensor(out=w_down[:, f, 0:D], in0=w_down[:, f, 0:D], scalar=gam[:, f, :], in1=ps[:, 4, 0:D],
                                         op0=ALU.mult, op1=ALU.subtract)
            dve.memset(w_down[:, :, D:D + 1], 1.0 / HID)
            dve.wait_ge(setup_mm, 3)
            dve.tensor_tensor(r_o, r_o, ps[:, 5, 0:D], ALU.add).then_inc(setup_done, 1)
            for name in PARTED[2:]:
                make_rest(name)

            def residue(g, bank, high_part, high_ready, ready):
                for c in range(C):
                    dve.wait_ge(high_ready, C * g + c + 1)
                    dve.tensor_tensor(fT_rest[:, c, :], ps[:, bank + c, :], high_part[:, c, :], ALU.subtract).then_inc(ready, 1)

            def stats(i, g, pairs, t):
                bs = slice(2 * pairs[0], 2 * pairs[-1] + 2)
                base = 5 * (2 * g + pairs[0])
                n = 2 * len(pairs)
                for b in range(bs.start, bs.stop):
                    dve.bn_stats(st[i][:, b, :], t[:, b, :]).then_inc(norm_step[i], 1)
                dve.wait_ge(norm_step[i], base + n)
                dve.memset(held[:], 0.0)
                for b in range(bs.start, bs.stop):
                    dve.bn_aggr(mv[i][:, b, :], st[i][:, b, :]).then_inc(norm_step[i], 1)
                dve.wait_ge(norm_step[i], base + 2 * n)
                dve.tensor_scalar(var[i][:, bs], mv[i][:, bs, 1], EPS, None, ALU.add).then_inc(norm_step[i], len(pairs))

            def scale(i, g, pairs, t, ready):
                dve.wait_ge(rstd_ready[i], 2 * g + pairs[-1] + 1)
                for b in range(2 * pairs[0], 2 * pairs[-1] + 2):
                    dve.tensor_scalar(t[:, b, :], t[:, b, :], mv[i][:, b, 0:1], rstd[i][:, b:b + 1], ALU.subtract,
                                      ALU.mult).then_inc(ready, 1)

            def x0_stats(g):
                dve.wait_ge(res0_ready, GB * g + GB)
                stats(0, g, (0, 1), x0)

            def x0_norm(g):
                scale(0, g, (0, 1), x0, x0_ready)

            def x1_stats(g):
                dve.wait_ge(res1_ready, 2 * g + 2)
                stats(1, g, (0, 1), x1)

            def x1_norm(g):
                scale(1, g, (0, 1), x1, x1_ready)

            def x2_stats(g):
                dve.wait_ge(res2_ready, 2 * g + 2)
                stats(2, g, (0, 1), x2)

            def x2_norm(g):
                scale(2, g, (0, 1), x2, x2_ready)

            def x3_stats(g, pair):
                dve.wait_ge(res3_ready, 2 * g + pair + 1)
                stats(3, g, (pair,), x3)

            def x3_norm(g, pair):
                scale(3, g, (pair,), x3, x3_ready)

            def att_exp(g):
                dve.wait_ge(adjA_in, 16 * g + 16)
                for b in range(GB):
                    dve.wait_ge(e0_ready, GB * g + b + 1)
                    dve.tensor_tensor(p0[:, b, :], e0[:, b, :], adjA[:, b, :], ALU.mult).then_inc(p0_ready, 1)

            def att_out(g, pair):
                dve.wait_ge(xb_ready, g + 1)
                for b in (2 * pair, 2 * pair + 1):
                    dve.wait_ge(att_done, GB * g + b + 1)
                    dve.reciprocal(rs0[:, b:b + 1], ps[:, att_bank(b), D:D + 1]).then_inc(rs0_ready, 1)
                    dve.wait_ge(rs0_ready, GB * g + b + 1)
                    dve.scalar_tensor_tensor(out=x0[:, b, :], in0=ps[:, att_bank(b), 0:D], scalar=rs0[:, b:b + 1], in1=x[:, b, :],
                                             op0=ALU.mult, op1=ALU.add).then_inc(res0_ready, 1)

            def gcn_3a(g, k):
                dve.wait_ge(gcn_done, 2 * g + k + 1)
                dve.wait_ge(x0b_ready, g + 1)
                bs = slice(2 * k, 2 * k + 2)
                dve.tensor_tensor(x1[:, bs, :], ps2[:, 2 + k], x0[:, bs, :], ALU.add).then_inc(res1_ready, 1)

            def mha_xt(g):
                residue(g, 6, x2T, x2T_ready, x2T_rest)

            def hyper_rest(g):
                residue(g, 6, gxT, gx_ready, gx_rest)

            def z_parts(g, z, done, count, full, ready):
                dve.wait_ge(done, count)
                for m in range(C):
                    dve.wait_ge(full, C * g + m + 1)
                    dve.tensor_copy(z_high[:, m, :], z[:, m, :]).then_inc(ready, 1)

            def z_rest(g, z, ready, rest_ready):
                dve.wait_ge(ready, C * g + C)
                dve.tensor_tensor(fT_rest[:], z[:], z_high[:], ALU.subtract).then_inc(rest_ready, 1)

            def gcn_1(g):
                z_parts(g, z1T, z1_done, C * g + C, z1_full, z1_ready)
                z_rest(g, z1T, z1_ready, z1_rest)

            def gcn_2a(g):
                z_parts(g, z2T, z2_done, g + 1, z2_full, z2_ready)
                z_rest(g, z2T, z2_ready, z2_rest)

            def up_high_part(g):
                for f in range(HC):
                    dve.wait_ge(up_ready, HC * g + f + 1)
                    last = dve.tensor_copy(up_high[:, f, :], upT[:, f, :])
                last.then_inc(up_high_ready, 1)

            def mha_ctx(g, pair):
                dve.wait_ge(ctx_ready, 2 * g + pair + 1)
                dve.tensor_tensor(ctx_rest[:].rearrange("p i b n -> p (i b) n"), ps4[:, 4 + 2 * pair],
                                  ctxT[:].rearrange("p i b n -> p (i b) n"), ALU.subtract).then_inc(ctx_rest_ready, 1)

            def gcn_ax(g):
                residue(g, 2, axT, ax_ready, ax_rest)

            def incidence(g):
                def step(k):
                    dve.wait_ge(inc_step, 4 * g + k)
                dve.wait_ge(adjTA_in, 16 * g + 16)
                dve.tensor_scalar(hT[:], adjTA[:], 0.0, None, ALU.not_equal).then_inc(inc_step, 1)
                dve.tensor_copy(bhT[:, :, P:P + 1], adjTA[:, :, 0:1])
                step(1)
                dve.tensor_reduce(cnt[:, 0, :], hT[:], AX.X, ALU.add).then_inc(inc_step, 1)
                step(2)
                dve.tensor_scalar(cnt[:, 1, :], cnt[:, 0, :], 1.0, None, ALU.max).then_inc(inc_step, 1)
                step(3)
                dve.reciprocal(cnt[:, 2, :], cnt[:, 1, :]).then_inc(inc_step, 1)
                step(4)
                dve.tensor_tensor(bhT[:, :, 0:P], hT[:], cnt[:, 2, :].unsqueeze(2).broadcast_to([P, GB, P]),
                                  ALU.mult).then_inc(inc_ready, 1)

            def degrees(g):
                def deg(k):
                    dve.wait_ge(degree_step, 6 * g + k)
                dve.wait_ge(gram_done, g + 1)
                d = [dn[:, i, :] for i in range(5)]
                for k in range(2):
                    pair = ps[:, k, 0:2 * (P + 1)].rearrange("p (b n) -> p b n", b=2)
                    dve.tensor_copy(dn[:, 0, 2 * k:2 * k + 2], pair[:, :, P]).then_inc(degree_step, 1)
                deg(2)
                dve.tensor_scalar(d[1], d[0], 0.0, None, ALU.is_gt).then_inc(degree_step, 1)
                deg(3)
                dve.tensor_scalar(d[2], d[1], 0.0, None, ALU.is_equal).then_inc(degree_step, 1)
                deg(4)
                dve.scalar_tensor_tensor(out=d[3], in0=d[0], scalar=0.0, in1=d[2], op0=ALU.max, op1=ALU.add).then_inc(degree_step, 1)
                deg(5)
                dve.reciprocal(d[4], d[3]).then_inc(degree_step, 1)

            def gram_scale(g):
                dve.wait_ge(degree_step, 6 * g + 6)
                for k in range(2):
                    for b in (2 * k, 2 * k + 1):
                        last = dve.tensor_scalar(gm[:, b, :], ps[:, k, (b % 2) * (P + 1):(b % 2) * (P + 1) + P],
                                                 dn[:, 4, b:b + 1], dn[:, 1, b:b + 1], ALU.mult, ALU.mult)
                    last.then_inc(gm_ready, 1)

            def hyper_down(g, half):
                def step(k):
                    dve.wait_ge(var_step, 8 * g + 4 * half + k)
                bs = slice(2 * half, 2 * half + 2)
                dve.wait_ge(down_done, GB * g + 2 * half + 2)
                for b in (2 * half, 2 * half + 1):
                    last = dve.tensor_copy(mom[:, b, :], ps[:, 4 + b, D:D + 2])
                last.then_inc(var_step, 1)
                step(1)
                dve.tensor_tensor(hv[:, 0, bs], mom[:, bs, 0], mom[:, bs, 0], ALU.mult).then_inc(var_step, 1)
                step(2)
                dve.tensor_tensor(hv[:, 1, bs], mom[:, bs, 1], hv[:, 0, bs], ALU.subtract).then_inc(var_step, 1)
                step(3)
                dve.tensor_scalar(hv[:, 2, bs], hv[:, 1, bs], 0.0, EPS, ALU.max, ALU.add).then_inc(var_step, 1)

            def squares(g):
                dve.wait_ge(sq_ready, 4 * g + 2)
                dve.tensor_tensor(sqs[:, 1, :], upT[:, 0, :], upT[:, 1, :], ALU.add).then_inc(sqs_step, 1)
                dve.wait_ge(sqs_step, 2 * g + 1)
                dve.wait_ge(sq_ready, 4 * g + 3)
                dve.tensor_tensor(sqs[:, 0, :], sqs[:, 1, :], upT[:, 2, :], ALU.add).then_inc(sqs_step, 1)
                dve.wait_ge(sqs_step, 2 * g + 2)
                dve.wait_ge(sq_ready, 4 * g + 4)
                dve.tensor_tensor(sqs[:, 0, :], sqs[:, 0, :], upT[:, 3, :], ALU.add).then_inc(sqs_ready, 1)

            def hyper_y(g, half):
                dve.wait_ge(h_rstd_ready, 2 * g + half + 1)
                for b in (2 * half, 2 * half + 1):
                    dve.scalar_tensor_tensor(out=y2[:, b, :], in0=ps[:, 4 + b, 0:D], scalar=hv[:, 3, b:b + 1],
                                             in1=r_down[:], op0=ALU.mult, op1=ALU.add).then_inc(y2_ready, 1)

            def hyper_out(g):
                for k in range(2):
                    dve.wait_ge(hyper_done, 2 * g + k + 1)
                    dve.wait_ge(x1d_ready, g + 1)
                    bs = slice(2 * k, 2 * k + 2)
                    dve.tensor_tensor(x2[:, bs, :], ps2[:, 4 + k], x1[:, bs, :], ALU.add).then_inc(res2_ready, 1)

            def mha_scores(g, pair):
                if pair == 0:
                    dve.wait_ge(adjB_in, 16 * g + 16)
                dve.wait_ge(s3h_done, 2 * g + pair + 1)
                for bb in range(2):
                    b = 2 * pair + bb
                    mask = adjB[:, b, :].unsqueeze(1).unsqueeze(1).broadcast_to([P, JR, C, P])
                    dve.tensor_tensor(pr[:, b].rearrange("p (j i) n -> p j i n", i=C), ps4[:, 4:8, 2 * bb:2 * bb + 2, :], mask,
                                      ALU.mult).then_inc(masked_ready, 1)

            def mha_max(g, b):
                dve.wait_ge(masked_ready, GB * g + b + 1)
                dve.tensor_reduce(mx[:, b, 0, :], pr[:, b], AX.X, ALU.max).then_inc(mx_step, 1)
                dve.wait_ge(mx_step, GB * g + b + 1)
                dve.tensor_scalar(mx[:, b, 1, :], mx[:, b, 0, :], -ATT, None, ALU.mult).then_inc(mx_ready, 1)

            def mha_div(g, b):
                dve.wait_ge(exp_ready, HEADS * (GB * g + b + 1))
                dve.reciprocal(den[:, b, 1, :], den[:, b, 0, :]).then_inc(den_step, 1)

            def mha_turn(g, b):
                dve.wait_ge(prT_done, GB * g + b + 1)
                dve.tensor_copy(prT[:, b % 2, 4:8, :], ps4[:, turn_bank(b) + 1]).then_inc(prT_dve, 1)

            def mha_wo(g, pair):
                dve.wait_ge(wo_done, 2 * g + pair + 1)
                if pair == 0 and not first(g):
                    dve.wait_ge(out_stored, 16 * g)
                dve.wait_ge(x2b_ready, g + 1)
                bs = slice(2 * pair, 2 * pair + 2)
                dve.tensor_tensor(x3[:, bs, :], ps2[:, 5 + 2 * pair], x2[:, bs, :], ALU.add).then_inc(res3_ready, 1)

            run(dve, {
                "att_exp": att_exp, "incidence": incidence, "degrees": degrees, "gram_scale": gram_scale,
                "att_out": lambda g: att_out(g, 0), "att_res1": lambda g: att_out(g, 1),
                "x3_stats0": lambda g: x3_stats(g, 0), "x3_stats1": lambda g: x3_stats(g, 1),
                "gcn_3a0": lambda g: gcn_3a(g, 0), "gcn_3a1": lambda g: gcn_3a(g, 1), "mha_xt": mha_xt,
                "hyper_rest": hyper_rest, "gcn_ax": gcn_ax, "gcn_1": gcn_1, "gcn_2a": gcn_2a,
                "up_high": up_high_part, "mha_ctx0": lambda g: mha_ctx(g, 0), "mha_ctx1": lambda g: mha_ctx(g, 1),
                "square_sum": squares, "hyper_y0": lambda g: hyper_y(g, 0), "hyper_y1": lambda g: hyper_y(g, 1),
                "hyper_down0": lambda g: hyper_down(g, 0), "hyper_down1": lambda g: hyper_down(g, 1),
                "hyper_out": hyper_out, "x0_stats": x0_stats, "x1_stats": x1_stats, "x2_stats": x2_stats,
                "x0_norm": x0_norm, "x1_norm": x1_norm, "x2_norm": x2_norm, "x3_norm0": lambda g: x3_norm(g, 0),
                "x3_norm1": lambda g: x3_norm(g, 1), "mha_scores0": lambda g: mha_scores(g, 0),
                "mha_scores1": lambda g: mha_scores(g, 1), "mha_max0": lambda g: mha_max(g, 0),
                "mha_max1": lambda g: mha_max(g, 1), "mha_max2": lambda g: mha_max(g, 2),
                "mha_max3": lambda g: mha_max(g, 3), "mha_div0": lambda g: mha_div(g, 0),
                "mha_div1": lambda g: mha_div(g, 1), "mha_div2": lambda g: mha_div(g, 2),
                "mha_div3": lambda g: mha_div(g, 3), "mha_turn0": lambda g: mha_turn(g, 0),
                "mha_turn1": lambda g: mha_turn(g, 1), "mha_turn2": lambda g: mha_turn(g, 2),
                "mha_turn3": lambda g: mha_turn(g, 3), "mha_wo0": lambda g: mha_wo(g, 0),
                "mha_wo1": lambda g: mha_wo(g, 1)})

        @block.gpsimd
        def _(pool):
            pool.memset(neg_half[:], -0.5)
            pool.memset(ident[:], 0.0).then_inc(ident_ready, 1)
            pool.wait_ge(ident_ready, 1)
            pool.affine_select(out=ident[:], in_=ident[:], compare_op=ALU.not_equal, fill=1.0, base=0, pattern=[[-1, P]],
                               channel_multiplier=1).then_inc(ident_ready, 1)
            pool.wait_ge(ident_ready, 2)

            def inv_sqrt(i, g, pairs):
                pool.wait_ge(norm_step[i], 5 * (2 * g + pairs[-1]) + 5)
                bs = slice(2 * pairs[0], 2 * pairs[-1] + 2)
                pool.tensor_tensor(rstd[i][:, bs], var[i][:, bs], neg_half[:, bs], ALU.pow).then_inc(rstd_ready[i], len(pairs))

            def att_t(g):
                pool.wait_ge(x_in, 16 * g + 16)
                pool.tensor_tensor(x[:], x[:], r_v0[:].unsqueeze(1).broadcast_to([P, GB, D]), ALU.add).then_inc(xb_ready, 1)

            def x0_stats(g):
                inv_sqrt(0, g, (0, 1))

            def x1_stats(g):
                inv_sqrt(1, g, (0, 1))

            def x2_stats(g):
                inv_sqrt(2, g, (0, 1))

            def x0_bias(g):
                pool.wait_ge(ax_done, g + 1)
                pool.tensor_tensor(x0[:], x0[:], r_g3[:].unsqueeze(1).broadcast_to([P, GB, D]), ALU.add).then_inc(x0b_ready, 1)

            def x1_twice(g):
                pool.wait_ge(gx_done, g + 1)
                pool.tensor_tensor(x1[:], x1[:], x1[:], ALU.add).then_inc(x1d_step, 1)
                pool.wait_ge(x1d_step, g + 1)
                pool.tensor_tensor(x1[:], x1[:], r_b2[:].unsqueeze(1).broadcast_to([P, GB, D]), ALU.add).then_inc(x1d_ready, 1)

            def up_rest_part(g, half):
                pool.wait_ge(up_high_ready, g + 1)
                fs = slice(2 * half, 2 * half + 2)
                pool.tensor_tensor(up_rest[:, fs, :], upT[:, fs, :], up_high[:, fs, :], ALU.subtract).then_inc(up_rest_ready, 1)

            def hyper_down(g, half):
                pool.wait_ge(var_step, 8 * g + 4 * half + 4)
                bs = slice(2 * half, 2 * half + 2)
                pool.tensor_tensor(hv[:, 3, bs], hv[:, 2, bs], neg_half[:, bs], ALU.pow).then_inc(h_rstd_ready, 1)

            def x3_stats(g, pair):
                inv_sqrt(3, g, (pair,))

            def x2_bias(g):
                pool.wait_ge(x2T_done, g + 1)
                pool.tensor_tensor(x2[:], x2[:], r_o[:].unsqueeze(1).broadcast_to([P, GB, D]), ALU.add).then_inc(x2b_ready, 1)

            def mha_div(g, b):
                pool.wait_ge(den_step, GB * g + b + 1)
                pool.tensor_tensor(pr[:, b], pr[:, b], den[:, b, 1, :].unsqueeze(2).broadcast_to([P, HEADS, P]),
                                   ALU.mult).then_inc(pr_ready, 1)

            def x_rest(g):
                pool.wait_ge(x_high_ready, g + 1)
                pool.tensor_tensor(xT_rest[:], xT[:], xT_high[:], ALU.subtract).then_inc(x_rest_ready, 1)

            def next_x_rest(g):
                if not final(g):
                    x_rest(g + 1)

            x_rest(0)
            pool.wait_ge(setup_done, 1)
            run(pool, {
                "x_rest": next_x_rest, "att_t": att_t, "x0_bias": x0_bias, "x2_bias": x2_bias, "x1_twice": x1_twice,
                "up_rest0": lambda g: up_rest_part(g, 0), "up_rest1": lambda g: up_rest_part(g, 1),
                "x0_stats": x0_stats, "x1_stats": x1_stats, "x2_stats": x2_stats,
                "x3_stats0": lambda g: x3_stats(g, 0), "x3_stats1": lambda g: x3_stats(g, 1),
                "hyper_down0": lambda g: hyper_down(g, 0), "hyper_down1": lambda g: hyper_down(g, 1),
                "mha_div0": lambda g: mha_div(g, 0), "mha_div1": lambda g: mha_div(g, 1),
                "mha_div2": lambda g: mha_div(g, 2), "mha_div3": lambda g: mha_div(g, 3)}, NG - 2)


def kernel(**inputs):
    import numpy as np
    import concourse.bacc as bacc
    from concourse.bass_utils import run_bass_kernel_spmd

    v = {k: np.asarray(a) for k, a in inputs.items()}
    x, adj = v["x"], v["adj"]
    n = x.shape[0] // GB

    def grouped(a):
        return np.ascontiguousarray(a.reshape(n, GB, *a.shape[1:]).transpose(0, 2, 1, 3))

    def filled(a, k):
        return np.concatenate([a, np.zeros((a.shape[0], k), a.dtype)], axis=1)

    w = {
        "Wq0": v["L0_gnn_Wq_w"], "Wk0": v["L0_gnn_Wk_w"], "Wv0T": filled(v["L0_gnn_Wv_w"].T, 2),
        "bq0": v["L0_gnn_Wq_b"], "bk0": v["L0_gnn_Wk_b"],
        "W1": v["L1_gnn_W1"], "W2": v["L1_gnn_W2"], "W3": v["L1_gnn_W3"], "b1": v["L1_gnn_b1"], "b2": v["L1_gnn_b2"],
        "WupT": v["L2_gnn_W1"].T, "bup": v["L2_gnn_b1"], "gamma": v["L2_gnn_gamma"], "beta": v["L2_gnn_beta"],
        "WdownT": filled(v["L2_gnn_W2"].T, 2),
        "Wqk3T": np.concatenate([v["L3_gnn_Wq"].T, v["L3_gnn_Wk"].T], axis=1),
        "bqk3": np.concatenate([v["L3_gnn_bq"], v["L3_gnn_bk"]]), "bv3": v["L3_gnn_bv"],
        "Wv3T": v["L3_gnn_Wv"].T, "WoT": v["L3_gnn_Wo"].T,
    }
    weights = np.concatenate(
        [w[name].reshape(c, P, m).transpose(1, 0, 2).reshape(P, c * m) for name, c, m in WEIGHTS], axis=1)
    rows = np.stack([v["L0_gnn_Wv_b"], v["L1_gnn_b3"], v["L2_gnn_b2"], v["L3_gnn_bo"]])
    xT = x.reshape(n, GB, P, C, P).transpose(0, 4, 3, 1, 2).reshape(n, P, C, N4)
    arrays = {"x": grouped(x), "xT": np.ascontiguousarray(xT), "adj": grouped(adj), "adjT": grouped(adj.transpose(0, 2, 1)),
              "weights": np.ascontiguousarray(weights), "rows": rows}

    nc = bacc.Bacc("TRN2", target_bir_lowering=False, num_devices=1)
    A = {k: nc.dram_tensor(f"in_{k}", a.shape, F32, kind="ExternalInput").ap() for k, a in arrays.items()}
    A["out"] = nc.dram_tensor("out_x", (n, P, GB, D), F32, kind="ExternalOutput").ap()
    build(nc, A)
    r = run_bass_kernel_spmd(nc, [{f"in_{k}": a for k, a in arrays.items()}], core_ids=[0])
    out = r.results[0]["out_x"]
    return out.transpose(0, 2, 1, 3).reshape(n * GB, P, D)
```
